# Optimizing a Trainium2 kernel written in Bass

```python
import numpy as np
import jax
import jax.numpy as jnp

def _softmax(x, axis=-1):
    return jax.nn.softmax(x, axis=axis)

def _gelu(x):
    return jax.nn.gelu(x, approximate=True)

def _silu(x):
    return jax.nn.silu(x)

def _sigmoid(x):
    return jax.nn.sigmoid(x)

def _layernorm(x, axis=-1, eps=1e-05):
    m = jnp.mean(x, axis=axis, keepdims=True)
    v = jnp.var(x, axis=axis, keepdims=True)
    return (x - m) / jnp.sqrt(v + eps)

def _scatter_add(tgt, idx, src, axis=0):
    return tgt.at[idx].add(src)

def _segment_sum(src, seg, n):
    return jax.ops.segment_sum(src, seg, n)
kernel_name = 'mk_cond_seq_d2_seqx_r4_ec9611'

def setup_inputs(seed: int=0):
    np.random.seed(seed)
    _w = jnp.asarray

    def _rec_inputs():
        import jax
        import jax.numpy as jnp
        _rk = jax.random.key(seed)
        x = -0.000125 + 0.9999 * jax.random.normal(jax.random.fold_in(_rk, 1), (128, 64, 256), jnp.float32)
        _lenS = 64 - jax.random.randint(jax.random.fold_in(_rk, 7), (128,), 0, max(1, 64 // 4) + 1, jnp.int32)
        _lenS2 = 64 - jax.random.randint(jax.random.fold_in(_rk, 8), (128,), 0, max(1, 64 // 4) + 1, jnp.int32)
        cond_256 = 0.000887014 + 1.03683 * jax.random.normal(jax.random.fold_in(_rk, 11), (128, 64), jnp.float32)
        return (x, cond_256)
    x, cond_256 = _rec_inputs()

    def _L0_cond_setup():
        import jax, jax.numpy as jnp
        import numpy as np
        EPS = 1e-05
        key = jax.random.key(seed)
        k1, k2, k3, k4 = jax.random.split(key, 4)
        b, t, d, num_con = (8, 1024, 256, 64)
        return {'input': jax.random.normal(k1, (b, t, d), dtype=jnp.float32), 'convInfo': jax.random.normal(k2, (b, num_con), dtype=jnp.float32), 'weight': jnp.ones((d,), dtype=jnp.float32), 'bias': jnp.zeros((d,), dtype=jnp.float32), 'lin_w': jax.random.normal(k3, (d, num_con), dtype=jnp.float32) * (1.0 / np.sqrt(num_con)), 'lin_b': jax.random.normal(k4, (d,), dtype=jnp.float32) * 0.01}
    _L0_cond_all = _L0_cond_setup()
    _L0_cond_in = {k: v for k, v in _L0_cond_all.items() if k in ('weight', 'bias', 'lin_w', 'lin_b')}
    del _L0_cond_all

    def _L1_cond_setup():
        import jax, jax.numpy as jnp
        import numpy as np
        from math import sqrt
        D_MODEL = 256
        N_HEADS = 16
        D_T = 64
        D_HID = 4 * D_MODEL
        EPS = 1e-06

        def _rmsnorm(x):
            return x * jax.lax.rsqrt(jnp.mean(x * x, axis=-1, keepdims=True) + EPS)

        def _ada_rmsnorm(x, t, gamma_w, beta_w):
            gamma = (t @ gamma_w.T)[:, None, :]
            beta = (t @ beta_w.T)[:, None, :]
            return gamma * _rmsnorm(x) + beta

        def _attention(x, W_q, W_k, W_v, W_o):
            b, l, dm = x.shape
            d_head = dm // N_HEADS
            scale = sqrt(N_HEADS / dm)

            def split(y):
                return y.reshape(b, l, N_HEADS, d_head).transpose(0, 2, 1, 3)
            q = split(x @ W_q.T)
            k = split(x @ W_k.T)
            v = split(x @ W_v.T)
            attn = jax.nn.softmax(scale * jnp.einsum('bnqd,bnkd->bnqk', q, k), axis=-1)
            o = jnp.einsum('bnqk,bnkd->bnqd', attn, v)
            o = o.transpose(0, 2, 1, 3).reshape(b, l, dm)
            return o @ W_o.T

        def _swiglu(x, gate_w, hidden_w, out_w, out_b):
            return jax.nn.silu(x @ gate_w.T) * (x @ hidden_w.T) @ out_w.T + out_b
        key = jax.random.key(seed)
        ks = jax.random.split(key, 16)
        s = 0.02
        inp = {'x': jax.random.normal(ks[0], (4, 512, D_MODEL), dtype=jnp.float32), 't': jax.random.normal(ks[1], (4, D_T), dtype=jnp.float32), 'attn_gamma_w': jax.random.normal(ks[2], (D_MODEL, D_T), dtype=jnp.float32) * s, 'attn_beta_w': jax.random.normal(ks[3], (D_MODEL, D_T), dtype=jnp.float32) * s, 'W_q': jax.random.normal(ks[4], (D_MODEL, D_MODEL), dtype=jnp.float32) * s, 'W_k': jax.random.normal(ks[5], (D_MODEL, D_MODEL), dtype=jnp.float32) * s, 'W_v': jax.random.normal(ks[6], (D_MODEL, D_MODEL), dtype=jnp.float32) * s, 'W_o': jax.random.normal(ks[7], (D_MODEL, D_MODEL), dtype=jnp.float32) * s, 'attn_alpha_w': jax.random.normal(ks[8], (D_MODEL, D_T), dtype=jnp.float32) * s, 'ffn_gamma_w': jax.random.normal(ks[9], (D_MODEL, D_T), dtype=jnp.float32) * s, 'ffn_beta_w': jax.random.normal(ks[10], (D_MODEL, D_T), dtype=jnp.float32) * s, 'gate_w': jax.random.normal(ks[11], (D_HID, D_MODEL), dtype=jnp.float32) * s, 'hidden_w': jax.random.normal(ks[12], (D_HID, D_MODEL), dtype=jnp.float32) * s, 'out_w': jax.random.normal(ks[13], (D_MODEL, D_HID), dtype=jnp.float32) * s, 'out_b': jnp.zeros((D_MODEL,), dtype=jnp.float32), 'ffn_alpha_w': jax.random.normal(ks[14], (D_MODEL, D_T), dtype=jnp.float32) * s}
        return inp
    _L1_cond_all = _L1_cond_setup()
    _L1_cond_in = {k: v for k, v in _L1_cond_all.items() if k in ('attn_gamma_w', 'attn_beta_w', 'W_q', 'W_k', 'W_v', 'W_o', 'attn_alpha_w', 'ffn_gamma_w', 'ffn_beta_w', 'gate_w', 'hidden_w', 'out_w', 'out_b', 'ffn_alpha_w')}
    del _L1_cond_all
    return {'x': x, 'cond_256': cond_256, 'L0_cond_weight': _L0_cond_in['weight'], 'L0_cond_bias': _L0_cond_in['bias'], 'L0_cond_lin_w': _L0_cond_in['lin_w'], 'L0_cond_lin_b': _L0_cond_in['lin_b'], 'L1_cond_attn_gamma_w': _L1_cond_in['attn_gamma_w'], 'L1_cond_attn_beta_w': _L1_cond_in['attn_beta_w'], 'L1_cond_W_q': _L1_cond_in['W_q'], 'L1_cond_W_k': _L1_cond_in['W_k'], 'L1_cond_W_v': _L1_cond_in['W_v'], 'L1_cond_W_o': _L1_cond_in['W_o'], 'L1_cond_attn_alpha_w': _L1_cond_in['attn_alpha_w'], 'L1_cond_ffn_gamma_w': _L1_cond_in['ffn_gamma_w'], 'L1_cond_ffn_beta_w': _L1_cond_in['ffn_beta_w'], 'L1_cond_gate_w': _L1_cond_in['gate_w'], 'L1_cond_hidden_w': _L1_cond_in['hidden_w'], 'L1_cond_out_w': _L1_cond_in['out_w'], 'L1_cond_out_b': _L1_cond_in['out_b'], 'L1_cond_ffn_alpha_w': _L1_cond_in['ffn_alpha_w']}

def reference(x, cond_256, L0_cond_weight, L0_cond_bias, L0_cond_lin_w, L0_cond_lin_b, L1_cond_attn_gamma_w, L1_cond_attn_beta_w, L1_cond_W_q, L1_cond_W_k, L1_cond_W_v, L1_cond_W_o, L1_cond_attn_alpha_w, L1_cond_ffn_gamma_w, L1_cond_ffn_beta_w, L1_cond_gate_w, L1_cond_hidden_w, L1_cond_out_w, L1_cond_out_b, L1_cond_ffn_alpha_w):
    import jax
    import jax.numpy as jnp

    def _L0_cond_ref(input, convInfo, weight, bias, lin_w, lin_b):
        import jax, jax.numpy as jnp
        import numpy as np
        EPS = 1e-05
        mean = jnp.mean(input, axis=-1, keepdims=True)
        var = jnp.mean(jnp.square(input - mean), axis=-1, keepdims=True)
        out = (input - mean) * jax.lax.rsqrt(var + EPS) * weight + bias
        tar_bias = jnp.tanh(convInfo @ lin_w.T + lin_b)[:, None, :]
        out = out + tar_bias
        return out * weight + bias

    def _L1_cond_ref(x, t, attn_gamma_w, attn_beta_w, W_q, W_k, W_v, W_o, attn_alpha_w, ffn_gamma_w, ffn_beta_w, gate_w, hidden_w, out_w, out_b, ffn_alpha_w):
        import jax, jax.numpy as jnp
        import numpy as np
        from math import sqrt
        D_MODEL = 256
        N_HEADS = 16
        D_T = 64
        D_HID = 4 * D_MODEL
        EPS = 1e-06

        def _rmsnorm(x):
            return x * jax.lax.rsqrt(jnp.mean(x * x, axis=-1, keepdims=True) + EPS)

        def _ada_rmsnorm(x, t, gamma_w, beta_w):
            gamma = (t @ gamma_w.T)[:, None, :]
            beta = (t @ beta_w.T)[:, None, :]
            return gamma * _rmsnorm(x) + beta

        def _attention(x, W_q, W_k, W_v, W_o):
            b, l, dm = x.shape
            d_head = dm // N_HEADS
            scale = sqrt(N_HEADS / dm)

            def split(y):
                return y.reshape(b, l, N_HEADS, d_head).transpose(0, 2, 1, 3)
            q = split(x @ W_q.T)
            k = split(x @ W_k.T)
            v = split(x @ W_v.T)
            attn = jax.nn.softmax(scale * jnp.einsum('bnqd,bnkd->bnqk', q, k), axis=-1)
            o = jnp.einsum('bnqk,bnkd->bnqd', attn, v)
            o = o.transpose(0, 2, 1, 3).reshape(b, l, dm)
            return o @ W_o.T

        def _swiglu(x, gate_w, hidden_w, out_w, out_b):
            return jax.nn.silu(x @ gate_w.T) * (x @ hidden_w.T) @ out_w.T + out_b
        a_alpha = (t @ attn_alpha_w.T)[:, None, :]
        x = x + a_alpha * _attention(_ada_rmsnorm(x, t, attn_gamma_w, attn_beta_w), W_q, W_k, W_v, W_o)
        f_alpha = (t @ ffn_alpha_w.T)[:, None, :]
        return x + f_alpha * _swiglu(_ada_rmsnorm(x, t, ffn_gamma_w, ffn_beta_w), gate_w, hidden_w, out_w, out_b)
    x = _L0_cond_ref(x, cond_256, L0_cond_weight, L0_cond_bias, L0_cond_lin_w, L0_cond_lin_b)
    x = _L1_cond_ref(x, cond_256, L1_cond_attn_gamma_w, L1_cond_attn_beta_w, L1_cond_W_q, L1_cond_W_k, L1_cond_W_v, L1_cond_W_o, L1_cond_attn_alpha_w, L1_cond_ffn_gamma_w, L1_cond_ffn_beta_w, L1_cond_gate_w, L1_cond_hidden_w, L1_cond_out_w, L1_cond_out_b, L1_cond_ffn_alpha_w)
    return x

_drawn_inputs = setup_inputs


def setup_inputs(seed=0):
    import zlib

    import numpy as np

    out = dict(_drawn_inputs(seed))
    spreads = {'L0_cond_weight': (1.0, 0.2), 'L0_cond_bias': (0.0, 0.1), 'L1_cond_out_b': (0.0, 0.686)}
    factors = {'L0_cond_lin_b': 8.0,
     'L1_cond_attn_gamma_w': 8.0,
     'L1_cond_attn_beta_w': 8.0,
     'L1_cond_W_q': 8.0,
     'L1_cond_W_k': 8.0,
     'L1_cond_W_v': 8.0,
     'L1_cond_W_o': 8.0,
     'L1_cond_attn_alpha_w': 8.0,
     'L1_cond_ffn_gamma_w': 8.0,
     'L1_cond_ffn_beta_w': 8.0,
     'L1_cond_gate_w': 8.0,
     'L1_cond_hidden_w': 8.0,
     'L1_cond_out_w': 8.0,
     'L1_cond_ffn_alpha_w': 4.878}
    for name, (base, spread) in spreads.items():
        noise = np.random.default_rng([zlib.crc32(name.encode()), seed]).standard_normal(out[name].shape)
        drawn = base * np.exp(spread * noise) if base else spread * noise
        out[name] = jnp.asarray(drawn.astype(out[name].dtype))
    for name, factor in factors.items():
        out[name] = (out[name] * factor).astype(out[name].dtype)
    return out
```

```python
from contextlib import ExitStack

import concourse.bass as bass
from concourse import mybir

ALU = mybir.AluOpType
ACT = mybir.ActivationFunctionType
F32 = mybir.dt.float32
F32R = mybir.dt.float32r
AX_X = mybir.AxisListType.X

P = 128
BATCH, SEQ, D = 128, 64, 256
HEADS, DH, HID, COND = 16, 16, 1024, 64
TOKENS = BATCH * SEQ
KT = D // P
HT = HID // P
BLK = 512
SEQS = BLK // SEQ
TILES = BLK // P
NBLK = TOKENS // BLK
HALF = P // 2
NC = 4
VW = 2 * DH + 1
SCALE = (HEADS / D) ** 0.5
LN_EPS, RMS_EPS = 1e-5, 1e-6
SHIFT, A_GAMMA, A_BETA, A_ALPHA, F_GAMMA, F_BETA, F_ALPHA = range(7)
WQ, WK, WV, WO = range(4)
LN_W, LN_B, LIN_B, OUT_B = range(4)


def over_blocks(eng, body):
    def pair(i):
        body(2 * i, i, 0)
        body(2 * i + 1, i, 1)

    pair(0)
    with eng.Fori(1, NBLK // 2 - 1) as i:
        pair(i)
    pair(NBLK // 2 - 1)


def reaches(n, least):
    return not isinstance(n, int) or n >= least


def exists(n):
    return not isinstance(n, int) or n < NBLK


def before(n, j, k):
    return (n, j - k) if j >= k else (n - 1, j - k + SEQS)


def conditioned_block(nc, x, cond_t, mod_w, feat_vecs, attn_w, gate_w, hidden_w, out_w, identity, head_mask, out_t):
    with ExitStack() as ctx:
        def sb(name, shape, dt=F32):
            return ctx.enter_context(nc.sbuf_tensor(name, shape, dt))

        def sem(name):
            return ctx.enter_context(nc.semaphore(name))

        bank = [ctx.enter_context(nc.psum_tensor(f"bank{i}", [P, BLK], F32)) for i in range(8)]

        x_res = sb("x_res", [P, KT, TOKENS])
        mod = sb("mod", [P, 7, KT, BATCH])
        vecs = sb("vecs", [P, 4, KT])
        w_sq = sb("w_sq", [P, KT])
        ident = sb("ident", [P, P])
        mean_w = sb("mean_w", [P, P])
        eps_ln = sb("eps_ln", [P, 1])
        eps_rms = sb("eps_rms", [P, 1])
        ffn_raw = sb("ffn_raw", [P, 3, KT * HID])

        loaded = sem("loaded")
        ffn_loaded = sem("ffn_loaded")
        consts_set = sem("consts_set")
        mod_ready = sem("mod_ready")
        resid1_done = sem("resid1_done")

        phase1(nc, ctx, bank, x, cond_t, mod_w, feat_vecs, attn_w, gate_w, hidden_w, out_w, identity, head_mask,
               x_res, mod, vecs, w_sq, ident, mean_w, eps_ln, eps_rms, ffn_raw,
               loaded, ffn_loaded, consts_set, mod_ready, resid1_done)
        phase2(nc, ctx, bank, x_res, mod, vecs, mean_w, eps_rms, ffn_raw, out_t)


def phase1(nc, outer, bank, x, cond_t, mod_w, feat_vecs, attn_w, gate_w, hidden_w, out_w, identity, head_mask,
           x_res, mod, vecs, w_sq, ident, mean_w, eps_ln, eps_rms, ffn_raw,
           loaded, ffn_loaded, consts_set, mod_ready, resid1_done):
    with ExitStack() as ctx:
        def sb(name, shape, dt=F32):
            return ctx.enter_context(nc.sbuf_tensor(name, shape, dt))

        def sem(name):
            return outer.enter_context(nc.semaphore(name))

        score_bank = bank[0:2]
        probs_bank, attended_bank, attT_bank = bank[2], bank[3], bank[4]
        work = bank[5:8]

        w_hi = sb("w_hi", [P, 4, KT, D], F32R)
        w_lo = sb("w_lo", [P, 4, KT, D], F32R)
        xin = [sb(f"xin{i}", [P, TILES, D]) for i in range(2)]
        stats = sb("stats", [P, TILES, 6])
        merge = sb("merge", [P, 4, TILES])
        mean = [sb(f"mean{i}", [P, TILES]) for i in range(2)]
        rstd = [sb(f"rstd{i}", [P, TILES]) for i in range(2)]
        squares = sb("squares", [P, KT, BLK])
        inv_rms = sb("inv_rms", [P, BLK])
        normed = sb("normed", [P, KT, BLK])
        xn_hi = sb("xn_hi", [P, KT, BLK], F32R)
        xn_lo = sb("xn_lo", [P, KT, BLK], F32R)
        keysT = [sb(f"keysT{i}", [P, KT, BLK]) for i in range(2)]
        k_heads = [sb(f"k_heads{i}", [P, KT, 4, SEQ]) for i in range(2)]
        q_diag = [sb(f"q_diag{i}", [P, KT, SEQS, P]) for i in range(2)]
        v_diag = [sb(f"v_diag{i}", [P, SEQS, 2 * NC, VW]) for i in range(2)]
        mask = sb("mask", [P, 4])
        row_max = [sb(f"row_max{i}", [P, 8]) for i in range(2)]
        probs = [sb(f"probs{i}", [P, 8 * SEQ]) for i in range(2)]
        probsT = [sb(f"probsT{i}", [P, NC * P]) for i in range(2)]
        inv_sum = [sb(f"inv_sum{i}", [P, NC * 2]) for i in range(2)]
        attended = [sb(f"attended{i}", [P, P]) for i in range(2)]
        att_hi = sb("att_hi", [P, 2, BLK], F32R)
        att_lo = sb("att_lo", [P, 2, BLK], F32R)
        gated = sb("gated", [P, KT, BLK])
        w_raw = q_diag[1]
        cond_sb = probs[0]

        x_loaded = [sem(f"x_loaded{i}") for i in range(2)]
        w_split = sem("w_split")
        diag_cleared = sem("diag_cleared")
        mod_mm = sem("mod_mm")
        mod_out = sem("mod_out")
        shift_made = sem("shift_made")
        stats_made = sem("stats_made")
        merged = sem("merged")
        v_cleared = sem("v_cleared")
        var_made = sem("var_made")
        std_made = sem("std_made")
        rstd_made = sem("rstd_made")
        x_normed = sem("x_normed")
        x_turned = sem("x_turned")
        res_made = sem("res_made")
        squared = sem("squared")
        ms_summed = sem("ms_summed")
        rms_made = sem("rms_made")
        inv_made = sem("inv_made")
        gamma_done = sem("gamma_done")
        scaled = sem("scaled")
        xn_made = sem("xn_made")
        xn_hi_made = sem("xn_hi_made")
        xn_lo_made = sem("xn_lo_made")
        k_mm, k_out = sem("k_mm"), sem("k_out")
        q_mm, q_out = sem("q_mm"), sem("q_out")
        v_mm, v_out = sem("v_mm"), sem("v_out")
        k_masked = sem("k_masked")
        scored = sem("scored")
        max_made = sem("max_made")
        centred = sem("centred")
        exp_made = sem("exp_made")
        probs_turned = sem("probs_turned")
        probsT_out = sem("probsT_out")
        summed = sem("summed")
        inv_sum_made = sem("inv_sum_made")
        att_normed = sem("att_normed")
        att_turned = sem("att_turned")
        att_hi_made = sem("att_hi_made")
        att_lo_made = sem("att_lo_made")
        wo_mm = sem("wo_mm")
        gated_made = sem("gated_made")

        block = ctx.enter_context(nc.Block())

        def seq_cols(table_row, kt, n):
            return mod[:, table_row, kt, bass.ds(n * SEQS, SEQS)].unsqueeze(2).broadcast_to([P, SEQS, SEQ])

        def by_seq(ap):
            return ap.rearrange("p (s t) -> p s t", t=SEQ)

        def res_block(kt, n):
            return x_res[:, kt, bass.ds(n * BLK, BLK)]

        @block.sync
        def _(sp):
            sp.dma_start(w_raw[:].rearrange("p a b c -> p (a b c)").rearrange("p (w k d) -> p w k d", w=4, k=KT),
                         attn_w.rearrange("w (k p) d -> p w k d", p=P)).then_inc(loaded, 16)
            sp.dma_start(vecs[:], feat_vecs).then_inc(loaded, 16)
            sp.dma_start(ident[:], identity).then_inc(loaded, 16)
            sp.dma_start(mask[:], head_mask).then_inc(loaded, 16)
            sp.dma_start(cond_sb[0:COND, 0:BATCH], cond_t).then_inc(loaded, 16)
            for i, rows in enumerate((range(0, 2), range(2, 4))):
                sp.dma_start(k_heads[i][0:COND].rearrange("p a b c -> p (a b c)").rearrange("p (w d) -> p w d", d=D),
                             mod_w[rows[0]:rows[-1] + 1].rearrange("w c d -> c w d")).then_inc(loaded, 16)
            sp.dma_start(probsT[0][0:COND].rearrange("p (w d) -> p w d", d=D),
                         mod_w[4:6].rearrange("w c d -> c w d")).then_inc(loaded, 16)
            sp.dma_start(probsT[1][0:COND, 0:D], mod_w[6]).then_inc(loaded, 16)

            def load_x(n, half, par):
                sp.dma_start(xin[par][:], x[bass.ds(n * BLK, BLK), :].rearrange("(t p) d -> p t d", p=P)
                             ).then_inc(x_loaded[par], 16)

            load_x(0, 0, 0)
            load_x(1, 0, 1)
            for i, w in enumerate((gate_w, hidden_w)):
                sp.dma_start(ffn_raw[:, i].rearrange("p (k h) -> p k h", k=KT),
                             w.rearrange("(k p) h -> p k h", p=P)).then_inc(ffn_loaded, 16)
            sp.dma_start(ffn_raw[:, 2].rearrange("p (t d) -> p t d", t=HT),
                         out_w.rearrange("(t p) d -> p t d", p=P)).then_inc(ffn_loaded, 16)
            with sp.Fori(0, NBLK // 2 - 1) as i:
                for par in range(2):
                    sp.wait_ge(x_turned, KT * (2 * i + par + 1))
                    load_x(2 * i + par + 2, i + 1, par)
            sp.wait_ge(ffn_loaded, 48)

        def mod_w_ap(row, kt):
            src = (k_heads[0][0:COND].rearrange("p a b c -> p (a b c)"), k_heads[1][0:COND].rearrange("p a b c -> p (a b c)"),
                   probsT[0][0:COND], probsT[1][0:COND])[row // 2]
            return src[:, (row % 2) * D + kt * P:(row % 2) * D + (kt + 1) * P]

        @block.tensor
        def _(pe):
            def three_pass(out, stat_hi, stat_lo, mov_hi, mov_lo, first, last):
                pe.matmul(out, stat_hi, mov_hi, start=first, stop=False)
                pe.matmul(out, stat_hi, mov_lo, start=False, stop=False)
                return pe.matmul(out, stat_lo, mov_hi, start=False, stop=last)

            def modulation():
                for i in range(7 * KT):
                    row, kt = i // KT, i % KT
                    mm = pe.matmul(bank[i // 4][:, (i % 4) * P:(i % 4 + 1) * P], mod_w_ap(row, kt),
                                   cond_sb[0:COND, 0:BATCH], start=True, stop=True)
                mm.then_inc(mod_mm, 1)

            def turn_x(m, par):
                pe.wait_ge(x_normed, m + 1)
                if reaches(m, 1):
                    pe.wait_ge(v_out, 2 * m)
                for kt in range(KT):
                    for t in range(TILES):
                        mm = pe.transpose(work[kt][:, t * P:(t + 1) * P], xin[par][:, t, kt * P:(kt + 1) * P], ident[:])
                    mm.then_inc(x_turned, 1)

            def mean_square(m):
                pe.wait_ge(squared, 2 * m + 2)
                if reaches(m, 1):
                    pe.wait_ge(q_out, 2 * m)
                for kt in range(KT):
                    mm = pe.matmul(work[2][:], mean_w[:], squares[:, kt], start=(kt == 0), stop=(kt == KT - 1))
                mm.then_inc(ms_summed, 1)

            def project(out, w, mt):
                for kt in range(KT):
                    mm = three_pass(out, w_hi[:, w, kt, mt * P:(mt + 1) * P], w_lo[:, w, kt, mt * P:(mt + 1) * P],
                                    xn_hi[:, kt], xn_lo[:, kt], kt == 0, kt == KT - 1)
                return mm

            def keys(m):
                pe.wait_ge(xn_lo_made, 2 * m + 2)
                pe.wait_ge(rms_made, m + 1)
                project(work[2][:], WK, 0).then_inc(k_mm, 1)
                if reaches(m, 2):
                    pe.wait_ge(gated_made, 2 * (m - 2) + 1)
                project(work[0][:], WK, 1).then_inc(k_mm, 1)

            def queries(m):
                if reaches(m, 2):
                    pe.wait_ge(gated_made, 2 * (m - 2) + 2)
                project(work[1][:], WQ, 0).then_inc(q_mm, 1)
                pe.wait_ge(k_out, 2 * m + 1)
                project(work[2][:], WQ, 1).then_inc(q_mm, 1)

            def values(m):
                for i in range(2):
                    if i == 0:
                        pe.wait_ge(k_out, 2 * m + 2)
                    else:
                        pe.wait_ge(q_out, 2 * m + 1)
                    for t in range(2):
                        tok = slice((2 * i + t) * P, (2 * i + t + 1) * P)
                        for kt in range(KT):
                            mm = three_pass(work[i][:, t * D:(t + 1) * D], xn_hi[:, kt, tok], xn_lo[:, kt, tok],
                                            w_hi[:, WV, kt], w_lo[:, WV, kt], kt == 0, kt == KT - 1)
                    mm.then_inc(v_mm, 1)

            def attention_out(b, mt):
                if mt == 0:
                    pe.wait_ge(att_lo_made, 2 * b + 2)
                for hh in range(2):
                    mm = three_pass(work[mt][:], w_hi[:, WO, hh, mt * P:(mt + 1) * P],
                                    w_lo[:, WO, hh, mt * P:(mt + 1) * P], att_hi[:, hh], att_lo[:, hh],
                                    hh == 0, hh == 1)
                mm.then_inc(wo_mm, 1)

            def score(n, j, par):
                g = SEQS * n + j
                pe.wait_ge(k_masked, g + 1)
                if j == 0:
                    pe.wait_ge(q_out, 2 * n + 2)
                if reaches(g, 2):
                    pe.wait_ge(centred, g - 1)
                for mt in range(KT):
                    mm = pe.matmul(score_bank[j % 2][:, mt * 256:(mt + 1) * 256], q_diag[par][:, mt, j],
                                   k_heads[j % 2][:, mt].rearrange("p h k -> p (h k)"), start=True, stop=True)
                mm.then_inc(scored, 1)

            def turn_probs(n, j):
                g = SEQS * n + j
                pe.wait_ge(exp_made, g + 1)
                if reaches(g, 1):
                    pe.wait_ge(probsT_out, g)
                for c in range(NC):
                    mm = pe.transpose(probs_bank[:, c * P:(c + 1) * P], probs[j % 2][:, c * P:(c + 1) * P], ident[:])
                mm.then_inc(probs_turned, 1)

            def times_values(n, j, par):
                g = SEQS * n + j
                pe.wait_ge(probsT_out, g + 1)
                if j == 0:
                    pe.wait_ge(v_out, 2 * n + 2)
                if reaches(g, 1):
                    pe.wait_ge(att_normed, g)
                for c in range(NC):
                    mm = pe.matmul(attended_bank[:, c * 2 * VW:(c + 1) * 2 * VW], probsT[j % 2][:, c * P:(c + 1) * P],
                                   v_diag[par][:, j, 2 * c:2 * c + 2].rearrange("p a b -> p (a b)"),
                                   start=True, stop=True)
                mm.then_inc(summed, 1)

            def turn_attended(n, j):
                pe.wait_ge(att_normed, SEQS * n + j + 1)
                if j % 4 == 0 and reaches(2 * n + j // 4, 1):
                    pe.wait_ge(att_lo_made, 2 * n + j // 4)
                pe.transpose(attT_bank[:, (j % 4) * P:(j % 4 + 1) * P], attended[j % 2][:], ident[:]
                             ).then_inc(att_turned, 1)

            def body(n, half, par):
                for j in range(SEQS):
                    score(n, j, par)
                    if reaches(SEQS * n + j, 1):
                        turn_probs(*before(n, j, 1))
                    if reaches(SEQS * n + j, 2):
                        turn_attended(*before(n, j, 2))
                    if exists(n + 1):
                        if j == 0:
                            turn_x(n + 1, 1 - par)
                        if j == 2:
                            mean_square(n + 1)
                        if j == 5:
                            keys(n + 1)
                        if j == 6:
                            queries(n + 1)
                        if j == 7:
                            values(n + 1)
                    if j in (3, 4) and reaches(n, 1):
                        attention_out(n - 1, j - 3)
                    if reaches(SEQS * n + j, 1):
                        times_values(*before(n, j, 1), par if j >= 1 else 1 - par)

            pe.wait_ge(loaded, 16 * 9)
            pe.wait_ge(consts_set, 1)
            modulation()
            pe.wait_ge(w_split, 2)
            turn_x(0, 0)
            mean_square(0)
            keys(0)
            queries(0)
            values(0)
            over_blocks(pe, body)
            turn_probs(NBLK - 1, SEQS - 1)
            turn_attended(NBLK - 1, SEQS - 2)
            times_values(NBLK - 1, SEQS - 1, 1)
            turn_attended(NBLK - 1, SEQS - 1)
            attention_out(NBLK - 1, 0)
            attention_out(NBLK - 1, 1)

        @block.vector
        def _(dve):
            def token_stats(m, half, par):
                dve.wait_ge(x_loaded[par], 16 * (half + 1))
                if reaches(m, 1):
                    dve.wait_ge(var_made, m)
                for t in range(TILES):
                    op = dve.bn_stats(stats[:, t], xin[par][:, t])
                op.then_inc(stats_made, 1)
                even_mean, odd_mean = stats[:, :, 1], stats[:, :, 4]
                dve.wait_ge(stats_made, m + 1)
                dve.tensor_tensor(merge[:, 0], even_mean, odd_mean, ALU.add)
                dve.tensor_tensor(merge[:, 1], even_mean, odd_mean, ALU.subtract)
                dve.tensor_tensor(merge[:, 2], stats[:, :, 2], stats[:, :, 5], ALU.add).then_inc(merged, 1)
                dve.wait_ge(merged, 2 * m + 1)
                dve.tensor_scalar(mean[par][:], merge[:, 0], 0.5, None, ALU.mult)
                dve.scalar_tensor_tensor(out=merge[:, 3], in0=merge[:, 1], scalar=0.25, in1=merge[:, 1],
                                         op0=ALU.mult, op1=ALU.mult).then_inc(merged, 1)
                dve.wait_ge(merged, 2 * m + 2)
                dve.scalar_tensor_tensor(out=rstd[par][:], in0=merge[:, 2], scalar=1.0 / D, in1=merge[:, 3],
                                         op0=ALU.mult, op1=ALU.add).then_inc(var_made, 1)

            def normalise_tokens(m, par):
                dve.wait_ge(std_made, m + 1)
                dve.reciprocal(rstd[par][:], rstd[par][:]).then_inc(rstd_made, 1)
                dve.wait_ge(rstd_made, m + 1)
                for t in range(TILES):
                    op = dve.tensor_scalar(xin[par][:, t], xin[par][:, t], mean[par][:, t:t + 1],
                                           rstd[par][:, t:t + 1], ALU.subtract, ALU.mult)
                op.then_inc(x_normed, 1)

            def make_residual(m):
                for kt in range(KT):
                    dve.wait_ge(x_turned, 2 * m + kt + 1)
                    dve.scalar_tensor_tensor(out=by_seq(res_block(kt, m)), in0=by_seq(work[kt][:]),
                                             scalar=w_sq[:, kt:kt + 1], in1=seq_cols(SHIFT, kt, m),
                                             op0=ALU.mult, op1=ALU.add).then_inc(res_made, 1)

            def invert_rms(m):
                dve.wait_ge(rms_made, m + 1)
                dve.reciprocal(inv_rms[:], inv_rms[:]).then_inc(inv_made, 1)

            def scale_by_rms(m):
                dve.wait_ge(inv_made, m + 1)
                for kt in range(KT):
                    dve.wait_ge(gamma_done, 2 * m + kt + 1)
                    dve.tensor_tensor(normed[:, kt], normed[:, kt], inv_rms[:], ALU.mult).then_inc(scaled, 1)

            def split_lo(m):
                if reaches(m, 1):
                    dve.wait_ge(v_mm, 2 * m)
                for kt in range(KT):
                    dve.wait_ge(xn_hi_made, 2 * m + kt + 1)
                    dve.tensor_tensor(xn_lo[:, kt], normed[:, kt], xn_hi[:, kt].bitcast(F32), ALU.subtract
                                      ).then_inc(xn_lo_made, 1)

            def centre(n, j):
                g = SEQS * n + j
                dve.wait_ge(scored, g + 1)
                dve.tensor_reduce(row_max[j % 2][:], score_bank[j % 2][:].rearrange("p (h k) -> p h k", k=SEQ),
                                  AX_X, ALU.max).then_inc(max_made, 1)
                if reaches(g, 2):
                    dve.wait_ge(probs_turned, g - 1)
                dve.wait_ge(max_made, g + 1)
                dve.tensor_tensor(probs[j % 2][:].rearrange("p (h k) -> p h k", k=SEQ),
                                  score_bank[j % 2][:].rearrange("p (h k) -> p h k", k=SEQ),
                                  row_max[j % 2][:].unsqueeze(2).broadcast_to([P, 8, SEQ]), ALU.subtract
                                  ).then_inc(centred, 1)

            def normalise_attended(n, j):
                g = SEQS * n + j
                dve.wait_ge(summed, g + 1)
                grid = attended_bank[:, 0:2 * NC * VW].rearrange("p (c h w) -> p c h w", h=2, w=VW)
                dve.reciprocal(inv_sum[j % 2][:].rearrange("p (c h) -> p c h", h=2), grid[:, :, :, VW - 1]
                               ).then_inc(inv_sum_made, 1)
                if reaches(g, 2):
                    dve.wait_ge(att_turned, g - 1)
                dve.wait_ge(inv_sum_made, g + 1)
                for hh in range(2):
                    rows = slice(hh * HALF, (hh + 1) * HALF)
                    op = dve.tensor_tensor(
                        attended[j % 2][rows].rearrange("p (c h d) -> p c h d", c=NC, d=DH),
                        grid[rows, :, hh, 0:2 * DH].rearrange("p c (h d) -> p c h d", d=DH),
                        inv_sum[j % 2][rows].rearrange("p (c h) -> p c h", h=2).unsqueeze(3)
                        .broadcast_to([HALF, NC, 2, DH]), ALU.mult)
                op.then_inc(att_normed, 1)

            def attended_lo(b, q):
                dve.wait_ge(att_hi_made, 2 * b + q + 1)
                cols = slice(q * BLK // 2, (q + 1) * BLK // 2)
                dve.tensor_tensor(att_lo[:, :, cols].rearrange("p h (s t) -> p h s t", t=SEQ),
                                  attT_bank[:].rearrange("p (s h t) -> p h s t", h=2, t=SEQ),
                                  att_hi[:, :, cols].bitcast(F32).rearrange("p h (s t) -> p h s t", t=SEQ),
                                  ALU.subtract).then_inc(att_lo_made, 1)

            def gate_attention(b, mt):
                dve.wait_ge(wo_mm, 2 * b + mt + 1)
                if reaches(b, 1):
                    dve.wait_ge(resid1_done, 2 * (b - 1) + mt + 1)
                dve.tensor_tensor(by_seq(gated[:, mt]), by_seq(work[mt][:]), seq_cols(A_ALPHA, mt, b), ALU.mult
                                  ).then_inc(gated_made, 1)

            def body(n, half, par):
                for j in range(SEQS):
                    centre(n, j)
                    if j == 0 and exists(n + 1):
                        make_residual(n + 1)
                    if j == 1 and reaches(n, 1):
                        attended_lo(n - 1, 1)
                    if j == 1 and exists(n + 2):
                        token_stats(n + 2, half + 1, par)
                    if j == 3 and exists(n + 1):
                        invert_rms(n + 1)
                        scale_by_rms(n + 1)
                    if j == 3 and exists(n + 2):
                        normalise_tokens(n + 2, par)
                    if j in (4, 5) and reaches(n, 1):
                        gate_attention(n - 1, j - 4)
                    if j == 4 and exists(n + 1):
                        split_lo(n + 1)
                    if j == 5:
                        attended_lo(n, 0)
                    if reaches(SEQS * n + j, 1):
                        normalise_attended(*before(n, j, 1))

            dve.wait_ge(loaded, 16 * 9)
            raw = w_raw[:].rearrange("p a b c -> p (a b c)")
            hi = w_hi[:].rearrange("p a b c -> p (a b c)")
            lo = w_lo[:].rearrange("p a b c -> p (a b c)")
            dve.tensor_copy(hi, raw).then_inc(w_split, 1)
            dve.wait_ge(w_split, 1)
            dve.tensor_tensor(lo, raw, hi.bitcast(F32), ALU.subtract).then_inc(w_split, 1)
            dve.tensor_tensor(w_sq[:], vecs[:, LN_W], vecs[:, LN_W], ALU.mult).then_inc(shift_made, 1)
            token_stats(0, 0, 0)
            dve.wait_ge(mod_out, 1)
            for kt in range(KT):
                op = dve.tensor_scalar(mod[:, SHIFT, kt], mod[:, SHIFT, kt], vecs[:, LN_B, kt:kt + 1],
                                       vecs[:, LN_W, kt:kt + 1], ALU.add, ALU.mult)
            op.then_inc(shift_made, 1)
            dve.wait_ge(shift_made, 2)
            for kt in range(KT):
                op = dve.tensor_scalar(mod[:, SHIFT, kt], mod[:, SHIFT, kt], vecs[:, LN_B, kt:kt + 1], None, ALU.add)
            op.then_inc(shift_made, 1)
            normalise_tokens(0, 0)
            dve.wait_ge(shift_made, 3)
            make_residual(0)
            token_stats(1, 0, 1)
            invert_rms(0)
            scale_by_rms(0)
            normalise_tokens(1, 1)
            split_lo(0)
            over_blocks(dve, body)
            normalise_attended(NBLK - 1, SEQS - 1)
            attended_lo(NBLK - 1, 1)
            gate_attention(NBLK - 1, 0)
            gate_attention(NBLK - 1, 1)

        @block.scalar
        def _(act):
            def square(m):
                if reaches(m, 1):
                    act.wait_ge(ms_summed, m)
                for kt in range(KT):
                    act.wait_ge(res_made, 2 * m + kt + 1)
                    act.activation(squares[:, kt], res_block(kt, m), ACT.Square).then_inc(squared, 1)

            def root_mean_square(m):
                act.wait_ge(ms_summed, m + 1)
                if reaches(m, 1):
                    act.wait_ge(scaled, 2 * m)
                act.activation(inv_rms[:], work[2][:], ACT.Sqrt, bias=eps_rms[:]).then_inc(rms_made, 1)

            def token_std(m, par):
                act.wait_ge(var_made, m + 1)
                act.activation(rstd[par][:], rstd[par][:], ACT.Sqrt, bias=eps_ln[:]).then_inc(std_made, 1)

            def split_hi(m):
                if reaches(m, 1):
                    act.wait_ge(v_mm, 2 * m)
                for kt in range(KT):
                    act.wait_ge(xn_made, 2 * m + kt + 1)
                    act.activation(xn_hi[:, kt], normed[:, kt], ACT.Copy).then_inc(xn_hi_made, 1)

            def keys_out(m, par):
                if reaches(m, 2):
                    act.wait_ge(k_masked, SEQS * (m - 1))
                for mt, bk in enumerate((2, 0)):
                    act.wait_ge(k_mm, 2 * m + mt + 1)
                    act.activation(keysT[par][:, mt], work[bk][:], ACT.Copy).then_inc(k_out, 1)

            def queries_out(m, par):
                if reaches(m, 2):
                    act.wait_ge(scored, SEQS * (m - 1))
                for mt, bk in enumerate((1, 2)):
                    act.wait_ge(q_mm, 2 * m + mt + 1)
                    for hh in range(2):
                        rows = slice(hh * HALF, (hh + 1) * HALF)
                        op = act.activation(q_diag[par][rows, mt, :, hh * SEQ:(hh + 1) * SEQ],
                                            by_seq(work[bk][rows]), ACT.Copy)
                    op.then_inc(q_out, 1)

            def values_out(m, par):
                if reaches(m, 2):
                    act.wait_ge(summed, SEQS * (m - 1))
                for i in range(2):
                    act.wait_ge(v_mm, 2 * m + i + 1)
                    for s in range(2):
                        for ho in range(2):
                            src = work[i][s * HALF:(s + 1) * HALF].rearrange("p (t c w) -> p t c w", t=2, w=2 * DH)
                            dst = v_diag[par][ho * HALF:(ho + 1) * HALF].rearrange(
                                "p (t s) c w -> p t s c w", s=2)
                            op = act.activation(dst[:, 2 * i:2 * i + 2, s, :, ho * DH:(ho + 1) * DH],
                                                src[:, :, :, ho * DH:(ho + 1) * DH], ACT.Copy)
                    op.then_inc(v_out, 1)

            def exponentials(n, j):
                g = SEQS * n + j
                act.wait_ge(centred, g + 1)
                act.activation(probs[j % 2][:], probs[j % 2][:], ACT.Exp, scale=SCALE).then_inc(exp_made, 1)

            def probs_out(n, j):
                g = SEQS * n + j
                act.wait_ge(probs_turned, g + 1)
                if reaches(g, 2):
                    act.wait_ge(summed, g - 1)
                act.activation(probsT[j % 2][:], probs_bank[:], ACT.Copy).then_inc(probsT_out, 1)

            def attended_hi(b, q):
                act.wait_ge(att_turned, SEQS * b + 4 * q + 4)
                if reaches(b, 1):
                    act.wait_ge(wo_mm, 2 * b)
                cols = slice(q * BLK // 2, (q + 1) * BLK // 2)
                act.activation(att_hi[:, :, cols].rearrange("p h (s t) -> p h s t", t=SEQ),
                               attT_bank[:].rearrange("p (s h t) -> p h s t", h=2, t=SEQ), ACT.Copy
                               ).then_inc(att_hi_made, 1)

            def body(n, half, par):
                for j in range(SEQS):
                    if reaches(SEQS * n + j, 1):
                        probs_out(*before(n, j, 1))
                    if j == 1 and reaches(n, 1):
                        attended_hi(n - 1, 1)
                    if j == 5:
                        attended_hi(n, 0)
                    if j == 1 and exists(n + 1):
                        square(n + 1)
                    exponentials(n, j)
                    if j == 2 and exists(n + 1):
                        root_mean_square(n + 1)
                    if j == 2 and exists(n + 2):
                        token_std(n + 2, par)
                    if exists(n + 1):
                        if j == 4:
                            split_hi(n + 1)
                        if j == 5:
                            keys_out(n + 1, 1 - par)
                        if j == 6:
                            queries_out(n + 1, 1 - par)
                        if j == 7:
                            values_out(n + 1, 1 - par)

            act.wait_ge(loaded, 16 * 9)
            act.wait_ge(mod_mm, 1)
            for kt in range(KT):
                act.activation(mod[:, SHIFT, kt], bank[0][:, kt * P:(kt + 1) * P], ACT.Tanh,
                               bias=vecs[:, LIN_B, kt:kt + 1])
            act.activation(mod[:, 1].rearrange("p k s -> p (k s)"), bank[0][:, 2 * P:4 * P], ACT.Copy)
            for i in range(1, 4):
                width = min(4 * P, 7 * KT * P - 4 * P * i)
                op = act.activation(mod[:].rearrange("p w k s -> p (w k s)")[:, 4 * P * i:4 * P * i + width],
                                    bank[i][:, 0:width], ACT.Copy)
            op.then_inc(mod_out, 1)
            act.wait_ge(consts_set, 1)
            act.wait_ge(diag_cleared, 1)
            token_std(0, 0)
            square(0)
            root_mean_square(0)
            token_std(1, 1)
            split_hi(0)
            keys_out(0, 0)
            queries_out(0, 0)
            values_out(0, 0)
            over_blocks(act, body)
            probs_out(NBLK - 1, SEQS - 1)
            attended_hi(NBLK - 1, 1)

        @block.gpsimd
        def _(pool):
            def apply_gamma(m):
                if reaches(m, 1):
                    pool.wait_ge(xn_lo_made, 2 * m)
                for kt in range(KT):
                    pool.wait_ge(res_made, 2 * m + kt + 1)
                    pool.tensor_tensor(by_seq(normed[:, kt]), by_seq(res_block(kt, m)), seq_cols(A_GAMMA, kt, m),
                                       ALU.mult).then_inc(gamma_done, 1)

            def apply_beta(m, kt):
                pool.wait_ge(scaled, 2 * m + kt + 1)
                pool.tensor_tensor(by_seq(normed[:, kt]), by_seq(normed[:, kt]), seq_cols(A_BETA, kt, m),
                                   ALU.add).then_inc(xn_made, 1)

            def mask_keys(m, j, par):
                g = SEQS * m + j
                if j == 0:
                    pool.wait_ge(k_out, 2 * m + 2)
                if reaches(g, 2):
                    pool.wait_ge(scored, g - 1)
                pool.tensor_tensor(k_heads[j % 2][:],
                                   keysT[par][:, :, j * SEQ:(j + 1) * SEQ].unsqueeze(2).broadcast_to([P, KT, 4, SEQ]),
                                   mask[:].unsqueeze(1).unsqueeze(3).broadcast_to([P, KT, 4, SEQ]), ALU.mult
                                   ).then_inc(k_masked, 1)

            def add_attention(b, mt):
                pool.wait_ge(gated_made, 2 * b + mt + 1)
                pool.tensor_tensor(res_block(mt, b), res_block(mt, b), gated[:, mt], ALU.add
                                   ).then_inc(resid1_done, 1)

            def body(n, half, par):
                for j in range(SEQS):
                    if j < SEQS - 1:
                        mask_keys(n, j + 1, par)
                    elif exists(n + 1):
                        mask_keys(n + 1, 0, 1 - par)
                    if j == 1 and exists(n + 1):
                        apply_gamma(n + 1)
                    if j == 3 and exists(n + 1):
                        apply_beta(n + 1, 0)
                        apply_beta(n + 1, 1)
                    if j in (4, 5) and reaches(n, 1):
                        add_attention(n - 1, j - 4)

            pool.memset(mean_w[:], 1.0 / D)
            pool.memset(eps_ln[:], LN_EPS)
            pool.memset(eps_rms[:], RMS_EPS).then_inc(consts_set, 1)
            pool.memset(q_diag[0][:], 0.0)
            for i in range(2):
                pool.memset(v_diag[i][:], 0.0).then_inc(v_cleared, 1)
            pool.wait_ge(v_cleared, 2)
            for i in range(2):
                grid = v_diag[i][:].rearrange("p s (c h) w -> p (s c) h w", h=2)
                for ho in range(2):
                    pool.memset(grid[ho * HALF:(ho + 1) * HALF, :, ho, VW - 1], 1.0).then_inc(v_cleared, 1)
                    pool.wait_ge(v_cleared, 2 + 2 * i + ho + 1)
            pool.wait_ge(w_split, 2)
            pool.memset(q_diag[1][:], 0.0).then_inc(diag_cleared, 1)
            pool.wait_ge(loaded, 16 * 9)
            pool.wait_ge(mod_out, 1)
            apply_gamma(0)
            apply_beta(0, 0)
            apply_beta(0, 1)
            pool.wait_ge(mod_mm, 1)
            mask_keys(0, 0, 0)
            over_blocks(pool, body)
            add_attention(NBLK - 1, 0)
            add_attention(NBLK - 1, 1)


def phase2(nc, outer, bank, x_res, mod, vecs, mean_w, eps_rms, ffn_raw, out_t):
    LAG = 2
    RING = 4
    with ExitStack() as ctx:
        def sb(name, shape, dt=F32):
            return ctx.enter_context(nc.sbuf_tensor(name, shape, dt))

        def sem(name):
            return outer.enter_context(nc.semaphore(name))

        gate_bank, hidden_bank, y_bank, ms_bank = bank[0:2], bank[2:4], bank[4:6], bank[6]

        w_hi = sb("ffn_hi", [P, 3, KT * HID], F32R)
        w_lo = sb("ffn_lo", [P, 3, KT * HID], F32R)
        squares = sb("squares2", [P, KT, BLK])
        inv_rms = sb("inv_rms2", [P, BLK])
        normed = sb("normed2", [P, KT, BLK])
        xn_hi = [sb(f"xn2_hi{i}", [P, KT, BLK], F32R) for i in range(2)]
        xn_lo = [sb(f"xn2_lo{i}", [P, KT, BLK], F32R) for i in range(2)]
        silu = [sb(f"silu{i}", [P, BLK]) for i in range(2)]
        prod = [sb(f"prod{i}", [P, BLK]) for i in range(2)]
        prod_hi = [sb(f"prod_hi{i}", [P, BLK], F32R) for i in range(RING)]
        prod_lo = [sb(f"prod_lo{i}", [P, BLK], F32R) for i in range(RING)]
        gated = sb("gated2", [P, KT, BLK])

        w_hi_made, w_lo_made = sem("ffn_hi_made"), sem("ffn_lo_made")
        squared = sem("squared2")
        ms_summed = sem("ms_summed2")
        rms_made = sem("rms_made2")
        inv_made = sem("inv_made2")
        gamma_done = sem("gamma_done2")
        scaled = sem("scaled2")
        xn_made = sem("xn_made2")
        xn_hi_made = sem("xn_hi_made2")
        xn_lo_made = sem("xn_lo_made2")
        gate_mm, hidden_mm = sem("gate_mm"), sem("hidden_mm")
        silu_made = sem("silu_made")
        prod_made = sem("prod_made")
        prod_hi_made = sem("prod_hi_made")
        prod_lo_made = sem("prod_lo_made")
        out_mm = sem("out_mm")
        gated_made = sem("gated_made2")
        y_made = sem("y_made")
        stored = sem("stored")

        block = ctx.enter_context(nc.Block())

        def seq_cols(table_row, kt, n):
            return mod[:, table_row, kt, bass.ds(n * SEQS, SEQS)].unsqueeze(2).broadcast_to([P, SEQS, SEQ])

        def by_seq(ap):
            return ap.rearrange("p (s t) -> p s t", t=SEQ)

        def res_block(kt, n):
            return x_res[:, kt, bass.ds(n * BLK, BLK)]

        @block.tensor
        def _(pe):
            def mean_square(m):
                pe.wait_ge(squared, 2 * m + 2)
                if reaches(m, 1):
                    pe.wait_ge(rms_made, m)
                for kt in range(KT):
                    mm = pe.matmul(ms_bank[:], mean_w[:], squares[:, kt], start=(kt == 0), stop=(kt == KT - 1))
                mm.then_inc(ms_summed, 1)

            def up(out, which, t, par):
                for kt in range(KT):
                    cols = slice(kt * HID + t * P, kt * HID + (t + 1) * P)
                    pe.matmul(out, w_hi[:, which, cols], xn_hi[par][:, kt], start=(kt == 0), stop=False)
                    pe.matmul(out, w_hi[:, which, cols], xn_lo[par][:, kt], start=False, stop=False)
                    mm = pe.matmul(out, w_lo[:, which, cols], xn_hi[par][:, kt], start=False, stop=(kt == KT - 1))
                return mm

            def down(n, t):
                pe.wait_ge(prod_lo_made, HT * n + t + 1)
                if t == 0 and reaches(n, 1):
                    pe.wait_ge(gated_made, 2 * n)
                for mt in range(KT):
                    cols = slice(t * D + mt * P, t * D + (mt + 1) * P)
                    pe.matmul(y_bank[mt][:], w_hi[:, 2, cols], prod_hi[t % RING][:], start=(t == 0), stop=False)
                    pe.matmul(y_bank[mt][:], w_hi[:, 2, cols], prod_lo[t % RING][:], start=False, stop=False)
                    mm = pe.matmul(y_bank[mt][:], w_lo[:, 2, cols], prod_hi[t % RING][:], start=False,
                                   stop=(t == HT - 1))
                mm.then_inc(out_mm, 1)

            def body(n, half, par):
                pe.wait_ge(xn_lo_made, 2 * n + 2)
                for t in range(HT):
                    early = not reaches(HT * n + t, 2)
                    if not early:
                        pe.wait_ge(silu_made, HT * n + t - 1)
                    up(gate_bank[t % 2][:], 0, t, par).then_inc(gate_mm, 1)
                    if not early:
                        pe.wait_ge(prod_made, HT * n + t - 1)
                    up(hidden_bank[t % 2][:], 1, t, par).then_inc(hidden_mm, 1)
                    if t >= LAG:
                        down(n, t - LAG)
                    elif reaches(n, 1):
                        down(n - 1, t - LAG + HT)
                    if t == 2 and exists(n + 1):
                        mean_square(n + 1)

            pe.wait_ge(w_lo_made, 3)
            mean_square(0)
            over_blocks(pe, body)
            down(NBLK - 1, HT - 2)
            down(NBLK - 1, HT - 1)

        @block.scalar
        def _(act):
            def square(m):
                if reaches(m, 1):
                    act.wait_ge(ms_summed, m)
                for kt in range(KT):
                    act.activation(squares[:, kt], res_block(kt, m), ACT.Square).then_inc(squared, 1)

            def root_mean_square(m):
                act.wait_ge(ms_summed, m + 1)
                if reaches(m, 1):
                    act.wait_ge(scaled, 2 * m)
                act.activation(inv_rms[:], ms_bank[:], ACT.Sqrt, bias=eps_rms[:]).then_inc(rms_made, 1)

            def split_hi(m, par):
                if reaches(m, 2):
                    act.wait_ge(hidden_mm, HT * (m - 1))
                for kt in range(KT):
                    act.wait_ge(xn_made, 2 * m + kt + 1)
                    act.activation(xn_hi[par][:, kt], normed[:, kt], ACT.Copy).then_inc(xn_hi_made, 1)

            def gate(n, t):
                act.wait_ge(gate_mm, HT * n + t + 1)
                if reaches(HT * n + t, 2):
                    act.wait_ge(prod_made, HT * n + t - 1)
                act.activation(silu[t % 2][:], gate_bank[t % 2][:], ACT.Silu).then_inc(silu_made, 1)

            def product_hi(n, t):
                act.wait_ge(prod_made, HT * n + t + 1)
                if reaches(HT * n + t, RING):
                    act.wait_ge(out_mm, HT * n + t - RING + 1)
                act.activation(prod_hi[t % RING][:], prod[t % 2][:], ACT.Copy).then_inc(prod_hi_made, 1)

            def body(n, half, par):
                for t in range(HT):
                    gate(n, t)
                    product_hi(n, t)
                    if t == 0 and exists(n + 1):
                        square(n + 1)
                    if t == 2 and exists(n + 1):
                        root_mean_square(n + 1)
                    if t == 4 and exists(n + 1):
                        split_hi(n + 1, 1 - par)

            for i in range(3):
                act.activation(w_hi[:, i], ffn_raw[:, i], ACT.Copy).then_inc(w_hi_made, 1)
            square(0)
            root_mean_square(0)
            split_hi(0, 0)
            over_blocks(act, body)

        @block.vector
        def _(dve):
            def invert_rms(m):
                dve.wait_ge(rms_made, m + 1)
                dve.reciprocal(inv_rms[:], inv_rms[:]).then_inc(inv_made, 1)
                dve.wait_ge(inv_made, m + 1)
                for kt in range(KT):
                    dve.wait_ge(gamma_done, 2 * m + kt + 1)
                    dve.tensor_tensor(normed[:, kt], normed[:, kt], inv_rms[:], ALU.mult).then_inc(scaled, 1)

            def split_lo(m, par):
                if reaches(m, 2):
                    dve.wait_ge(hidden_mm, HT * (m - 1))
                for kt in range(KT):
                    dve.wait_ge(xn_hi_made, 2 * m + kt + 1)
                    dve.tensor_tensor(xn_lo[par][:, kt], normed[:, kt], xn_hi[par][:, kt].bitcast(F32),
                                      ALU.subtract).then_inc(xn_lo_made, 1)

            def product(n, t):
                dve.wait_ge(silu_made, HT * n + t + 1)
                dve.wait_ge(hidden_mm, HT * n + t + 1)
                if reaches(HT * n + t, 2):
                    dve.wait_ge(prod_lo_made, HT * n + t - 1)
                dve.tensor_tensor(prod[t % 2][:], hidden_bank[t % 2][:], silu[t % 2][:], ALU.mult
                                  ).then_inc(prod_made, 1)

            def product_lo(n, t):
                dve.wait_ge(prod_hi_made, HT * n + t + 1)
                if reaches(HT * n + t, RING):
                    dve.wait_ge(out_mm, HT * n + t - RING + 1)
                dve.tensor_tensor(prod_lo[t % RING][:], prod[t % 2][:], prod_hi[t % RING][:].bitcast(F32),
                                  ALU.subtract).then_inc(prod_lo_made, 1)

            def gate_ffn(b):
                dve.wait_ge(out_mm, HT * (b + 1))
                if reaches(b, 1):
                    dve.wait_ge(y_made, 2 * b)
                for mt in range(KT):
                    dve.scalar_tensor_tensor(out=by_seq(gated[:, mt]), in0=by_seq(y_bank[mt][:]),
                                             scalar=vecs[:, OUT_B, mt:mt + 1], in1=seq_cols(F_ALPHA, mt, b),
                                             op0=ALU.add, op1=ALU.mult).then_inc(gated_made, 1)

            def body(n, half, par):
                for t in range(HT):
                    product(n, t)
                    product_lo(n, t)
                    if t == 1 and reaches(n, 1):
                        gate_ffn(n - 1)
                    if t == 3 and exists(n + 1):
                        invert_rms(n + 1)
                    if t == 4 and exists(n + 1):
                        split_lo(n + 1, 1 - par)

            for i in range(3):
                dve.wait_ge(w_hi_made, i + 1)
                dve.tensor_tensor(w_lo[:, i], ffn_raw[:, i], w_hi[:, i].bitcast(F32), ALU.subtract
                                  ).then_inc(w_lo_made, 1)
            invert_rms(0)
            split_lo(0, 0)
            over_blocks(dve, body)
            gate_ffn(NBLK - 1)

        @block.gpsimd
        def _(pool):
            def apply_gamma(m):
                if reaches(m, 1):
                    pool.wait_ge(xn_lo_made, 2 * m)
                for kt in range(KT):
                    pool.tensor_tensor(by_seq(normed[:, kt]), by_seq(res_block(kt, m)), seq_cols(F_GAMMA, kt, m),
                                       ALU.mult).then_inc(gamma_done, 1)

            def apply_beta(m):
                for kt in range(KT):
                    pool.wait_ge(scaled, 2 * m + kt + 1)
                    pool.tensor_tensor(by_seq(normed[:, kt]), by_seq(normed[:, kt]), seq_cols(F_BETA, kt, m),
                                       ALU.add).then_inc(xn_made, 1)

            def add_ffn(b):
                for mt in range(KT):
                    pool.wait_ge(gated_made, 2 * b + mt + 1)
                    pool.tensor_tensor(res_block(mt, b), res_block(mt, b), gated[:, mt], ALU.add
                                       ).then_inc(y_made, 1)

            def body(n, half, par):
                if exists(n + 1):
                    apply_gamma(n + 1)
                if reaches(n, 1):
                    add_ffn(n - 1)
                if exists(n + 1):
                    apply_beta(n + 1)

            apply_gamma(0)
            apply_beta(0)
            over_blocks(pool, body)
            add_ffn(NBLK - 1)

        @block.sync
        def _(sp):
            def store(n):
                for kt in range(KT):
                    sp.wait_ge(y_made, 2 * n + kt + 1)
                    sp.dma_start(out_t[kt * P:(kt + 1) * P, bass.ds(n * BLK, BLK)], res_block(kt, n)
                                 ).then_inc(stored, 16)

            with sp.Fori(0, NBLK) as n:
                store(n)
            sp.wait_ge(stored, 16 * KT * NBLK)


def kernel(**inputs):
    import numpy as np
    import concourse.bacc as bacc
    from concourse import mybir as mb
    from concourse.bass_utils import run_bass_kernel_spmd

    a = {k: np.asarray(v) for k, v in inputs.items()}
    f = {k[len("L1_cond_"):]: v for k, v in a.items() if k.startswith("L1_cond_")}
    by_partition = lambda v: v.reshape(KT, P).T
    split_heads = lambda w: w.reshape(2, 2, 2, 2, DH, D)
    wv = split_heads(f["W_v"]).transpose(0, 2, 1, 3, 4, 5).reshape(D, D)
    wo = split_heads(f["W_o"].T).transpose(1, 0, 2, 3, 4, 5).reshape(D, D)
    mod_rows = [a["L0_cond_lin_w"], f["attn_gamma_w"], f["attn_beta_w"], f["attn_alpha_w"],
                f["ffn_gamma_w"], f["ffn_beta_w"], f["ffn_alpha_w"]]
    features = np.arange(P)
    arrays = {
        "x": a["x"].reshape(TOKENS, D),
        "cond_t": a["cond_256"].T,
        "mod_w": np.stack([w.T for w in mod_rows]),
        "feat_vecs": np.stack([by_partition(v) for v in
                               (a["L0_cond_weight"], a["L0_cond_bias"], a["L0_cond_lin_b"], f["out_b"])], axis=1),
        "attn_w": np.stack([f["W_q"].T, f["W_k"].T, wv.T, wo]),
        "gate_w": f["gate_w"].T,
        "hidden_w": f["hidden_w"].T,
        "out_w": f["out_w"].T,
        "identity": np.eye(P, dtype=np.float32),
        "head_mask": (features[:, None] % HALF // DH == np.arange(4)[None, :]).astype(np.float32),
    }
    nc = bacc.Bacc("TRN2", target_bir_lowering=False, num_devices=1)
    args, feeds = [], {}
    for name, v in arrays.items():
        v = np.ascontiguousarray(v)
        feeds[f"{name}_dram"] = v
        args.append(nc.dram_tensor(f"{name}_dram", v.shape, mb.dt.from_np(v.dtype), kind="ExternalInput").ap())
    args.append(nc.dram_tensor("out_t_dram", (D, TOKENS), F32, kind="ExternalOutput").ap())
    conditioned_block(nc, *args)
    r = run_bass_kernel_spmd(nc, [feeds], core_ids=[0])
    got = r.results[0]["out_t_dram"]
    return np.ascontiguousarray(got.T).reshape(BATCH, SEQ, D)
```

```python
from contextlib import ExitStack

import concourse.bass as bass
from concourse import mybir

ALU = mybir.AluOpType
ACT = mybir.ActivationFunctionType
F32 = mybir.dt.float32
F32R = mybir.dt.float32r
AX_X = mybir.AxisListType.X

P = 128
BATCH, SEQ, D = 128, 64, 256
HEADS, DH, HID, COND = 16, 16, 1024, 64
TOKENS = BATCH * SEQ
KT = D // P
HT = HID // P
BLK = 512
SEQS = BLK // SEQ
TILES = BLK // P
NBLK = TOKENS // BLK
HALF = P // 2
NC = 4
VW = 2 * DH + 1
SCALE = (HEADS / D) ** 0.5
LN_EPS, RMS_EPS = 1e-5, 1e-6
SHIFT, A_GAMMA, A_BETA, A_ALPHA, F_GAMMA, F_BETA, F_ALPHA = range(7)
WQ, WK, WV, WO = range(4)
LN_W, LN_B, LIN_B, OUT_B = range(4)


def over_blocks(eng, body):
    def pair(i):
        body(2 * i, i, 0)
        body(2 * i + 1, i, 1)

    pair(0)
    with eng.Fori(1, NBLK // 2 - 1) as i:
        pair(i)
    pair(NBLK // 2 - 1)


def reaches(n, least):
    return not isinstance(n, int) or n >= least


def exists(n):
    return not isinstance(n, int) or n < NBLK


def before(n, j, k):
    return (n, j - k) if j >= k else (n - 1, j - k + SEQS)


def conditioned_block(nc, x, cond_t, mod_w, feat_vecs, attn_w, gate_w, hidden_w, out_w, identity, head_mask, out_t):
    with ExitStack() as ctx:
        def sb(name, shape, dt=F32):
            return ctx.enter_context(nc.sbuf_tensor(name, shape, dt))

        def sem(name):
            return ctx.enter_context(nc.semaphore(name))

        bank = [ctx.enter_context(nc.psum_tensor(f"bank{i}", [P, BLK], F32)) for i in range(8)]

        x_res = sb("x_res", [P, KT, TOKENS])
        mod = sb("mod", [P, 7, KT, BATCH])
        vecs = sb("vecs", [P, 4, KT])
        w_sq = sb("w_sq", [P, KT])
        ident = sb("ident", [P, P])
        ones = sb("ones", [P, P])
        mean_col = sb("mean_col", [P, 1])
        mean_w = sb("mean_w", [P, P], F32R)
        eps_rms = sb("eps_rms", [P, 1])
        normed = sb("normed", [P, KT, BLK])
        xn_hi = sb("xn_hi", [P, KT, BLK], F32R)
        xn_lo = sb("xn_lo", [P, KT, BLK], F32R)
        ffn_raw = sb("ffn_raw", [P, 3, KT * HID])

        loaded = sem("loaded")
        ffn_loaded = sem("ffn_loaded")
        consts_set = sem("consts_set")
        resid1_done = sem("resid1_done")

        phase1(nc, ctx, bank, x, cond_t, mod_w, feat_vecs, attn_w, gate_w, hidden_w, out_w, identity, head_mask,
               x_res, mod, vecs, w_sq, ident, ones, mean_col, mean_w, eps_rms, normed, xn_hi, xn_lo, ffn_raw,
               loaded, ffn_loaded, consts_set, resid1_done)
        phase2(nc, ctx, bank, x_res, mod, vecs, mean_w, eps_rms, normed, xn_hi, xn_lo, ffn_raw, out_t)


def phase1(nc, outer, bank, x, cond_t, mod_w, feat_vecs, attn_w, gate_w, hidden_w, out_w, identity, head_mask,
           x_res, mod, vecs, w_sq, ident, ones, mean_col, mean_w, eps_rms, normed, xn_hi, xn_lo, ffn_raw,
           loaded, ffn_loaded, consts_set, resid1_done):
    with ExitStack() as ctx:
        def sb(name, shape, dt=F32):
            return ctx.enter_context(nc.sbuf_tensor(name, shape, dt))

        def sem(name):
            return outer.enter_context(nc.semaphore(name))

        score_bank = bank[0:2]
        probs_bank, attended_bank, attT_bank = bank[2], bank[3], bank[4]
        work = bank[5:8]

        w_hi = sb("w_hi", [P, 4, KT, D], F32R)
        w_lo = sb("w_lo", [P, 4, KT, D], F32R)
        xin = [sb(f"xin{i}", [P, TILES, D]) for i in range(2)]
        stats = sb("stats", [P, TILES, 6])
        merge = sb("merge", [P, 5, TILES])
        mean = [sb(f"mean{i}", [P, TILES]) for i in range(2)]
        rstd = [sb(f"rstd{i}", [P, TILES]) for i in range(2)]
        squares = sb("squares", [P, KT, BLK])
        mean_sq = sb("mean_sq", [P, TILES])
        inv_diag = sb("inv_diag", [P, TILES, P])
        minus_half = sb("minus_half", [P, TILES])
        keysT = [sb(f"keysT{i}", [P, KT, BLK]) for i in range(2)]
        k_heads = [sb(f"k_heads{i}", [P, KT, 4, SEQ]) for i in range(2)]
        q_diag = [sb(f"q_diag{i}", [P, KT, SEQS, P]) for i in range(2)]
        v_diag = sb("v_diag", [P, SEQS, 2 * NC, VW])
        mask = sb("mask", [P, 4])
        row_max = [sb(f"row_max{i}", [P, 8]) for i in range(2)]
        probs = [sb(f"probs{i}", [P, 8 * SEQ]) for i in range(2)]
        probsT = [sb(f"probsT{i}", [P, NC * P]) for i in range(2)]
        inv_sum = [sb(f"inv_sum{i}", [P, NC * 2]) for i in range(2)]
        attended = [sb(f"attended{i}", [P, P]) for i in range(2)]
        att_hi = sb("att_hi", [P, 2, BLK], F32R)
        att_lo = sb("att_lo", [P, 2, BLK], F32R)
        gated = sb("gated", [P, KT, BLK])
        w_raw = q_diag[1]
        cond_sb = probs[0]

        x_loaded = [sem(f"x_loaded{i}") for i in range(2)]
        w_split = sem("w_split")
        diag_cleared = sem("diag_cleared")
        mod_mm = sem("mod_mm")
        mod_out = sem("mod_out")
        shift_made = sem("shift_made")
        stats_made = sem("stats_made")
        merged = sem("merged")
        v_cleared = sem("v_cleared")
        var_made = sem("var_made")
        rstd_made = sem("rstd_made")
        x_normed = sem("x_normed")
        x_turned = sem("x_turned")
        res_made = sem("res_made")
        squared = sem("squared")
        ms_summed = sem("ms_summed")
        ms_out = sem("ms_out")
        inv_made = sem("inv_made")
        diag_made = sem("diag_made")
        inv_spread = sem("inv_spread")
        gamma_done = sem("gamma_done")
        scaled = sem("scaled")
        xn_made = sem("xn_made")
        xn_hi_made = sem("xn_hi_made")
        xn_lo_made = sem("xn_lo_made")
        k_mm, k_out = sem("k_mm"), sem("k_out")
        q_mm, q_out = sem("q_mm"), sem("q_out")
        v_mm, v_out = sem("v_mm"), sem("v_out")
        k_masked = sem("k_masked")
        scored = sem("scored")
        max_made = sem("max_made")
        centred = sem("centred")
        exp_made = sem("exp_made")
        probs_turned = sem("probs_turned")
        probsT_out = sem("probsT_out")
        summed = sem("summed")
        inv_sum_made = sem("inv_sum_made")
        att_normed = sem("att_normed")
        att_turned = sem("att_turned")
        att_hi_made = sem("att_hi_made")
        att_lo_made = sem("att_lo_made")
        wo_mm = sem("wo_mm")
        gated_made = sem("gated_made")

        block = ctx.enter_context(nc.Block())

        def seq_cols(table_row, kt, n):
            return mod[:, table_row, kt, bass.ds(n * SEQS, SEQS)].unsqueeze(2).broadcast_to([P, SEQS, SEQ])

        def by_seq(ap):
            return ap.rearrange("p (s t) -> p s t", t=SEQ)

        def res_block(kt, n):
            return x_res[:, kt, bass.ds(n * BLK, BLK)]

        def normed_block(m):
            return 0 if isinstance(m, int) and m == NBLK else m

        def row_for(m, attn_row, ffn_row):
            return ffn_row if isinstance(m, int) and m == NBLK else attn_row

        @block.sync
        def _(sp):
            sp.dma_start(w_raw[:].rearrange("p a b c -> p (a b c)").rearrange("p (w k d) -> p w k d", w=4, k=KT),
                         attn_w.rearrange("w (k p) d -> p w k d", p=P)).then_inc(loaded, 16)
            sp.dma_start(vecs[:], feat_vecs).then_inc(loaded, 16)
            sp.dma_start(ident[:], identity).then_inc(loaded, 16)
            sp.dma_start(mask[:], head_mask).then_inc(loaded, 16)
            sp.dma_start(cond_sb[0:COND, 0:BATCH], cond_t).then_inc(loaded, 16)
            for i, rows in enumerate((range(0, 2), range(2, 4))):
                sp.dma_start(k_heads[i][0:COND].rearrange("p a b c -> p (a b c)").rearrange("p (w d) -> p w d", d=D),
                             mod_w[rows[0]:rows[-1] + 1].rearrange("w c d -> c w d")).then_inc(loaded, 16)
            sp.dma_start(probsT[0][0:COND].rearrange("p (w d) -> p w d", d=D),
                         mod_w[4:6].rearrange("w c d -> c w d")).then_inc(loaded, 16)
            sp.dma_start(probsT[1][0:COND, 0:D], mod_w[6]).then_inc(loaded, 16)

            def load_x(n, half, par):
                sp.dma_start(xin[par][:], x[bass.ds(n * BLK, BLK), :].rearrange("(t p) d -> p t d", p=P)
                             ).then_inc(x_loaded[par], 16)

            load_x(0, 0, 0)
            load_x(1, 0, 1)
            for i, w in enumerate((gate_w, hidden_w)):
                sp.dma_start(ffn_raw[:, i].rearrange("p (k h) -> p k h", k=KT),
                             w.rearrange("(k p) h -> p k h", p=P)).then_inc(ffn_loaded, 16)
            sp.dma_start(ffn_raw[:, 2].rearrange("p (t d) -> p t d", t=HT),
                         out_w.rearrange("(t p) d -> p t d", p=P)).then_inc(ffn_loaded, 16)
            with sp.Fori(0, NBLK // 2 - 1) as i:
                for par in range(2):
                    sp.wait_ge(x_turned, KT * (2 * i + par + 1))
                    load_x(2 * i + par + 2, i + 1, par)
            sp.wait_ge(ffn_loaded, 48)

        def mod_w_ap(row, kt):
            src = (k_heads[0][0:COND].rearrange("p a b c -> p (a b c)"),
                   k_heads[1][0:COND].rearrange("p a b c -> p (a b c)"),
                   probsT[0][0:COND], probsT[1][0:COND])[row // 2]
            return src[:, (row % 2) * D + kt * P:(row % 2) * D + (kt + 1) * P]

        @block.tensor
        def _(pe):
            def three_pass(out, stat_hi, stat_lo, mov_hi, mov_lo, first, last):
                pe.matmul(out, stat_hi, mov_hi, start=first, stop=False)
                pe.matmul(out, stat_hi, mov_lo, start=False, stop=False)
                return pe.matmul(out, stat_lo, mov_hi, start=False, stop=last)

            def modulation():
                for i in range(7 * KT):
                    row, kt = i // KT, i % KT
                    mm = pe.matmul(bank[i // 4][:, (i % 4) * P:(i % 4 + 1) * P], mod_w_ap(row, kt),
                                   cond_sb[0:COND, 0:BATCH], start=True, stop=True)
                mm.then_inc(mod_mm, 1)

            def turn_x(m, par, kt):
                pe.wait_ge(x_normed, m + 1)
                for t in range(TILES):
                    mm = pe.transpose(work[(2, 0)[kt]][:, t * P:(t + 1) * P], xin[par][:, t, kt * P:(kt + 1) * P],
                                      ident[:])
                mm.then_inc(x_turned, 1)

            def mean_square(m):
                pe.wait_ge(squared, 2 * m + 2)
                for t in range(TILES):
                    for kt in range(KT):
                        mm = pe.matmul(work[0][:, t:t + 1], squares[:, kt, t * P:(t + 1) * P], mean_col[:],
                                       start=(kt == 0), stop=(kt == KT - 1))
                mm.then_inc(ms_summed, 1)

            def spread_inverse(m):
                pe.wait_ge(diag_made, m + 1)
                pe.matmul(work[2][:], ones[:], inv_diag[:].rearrange("p t q -> p (t q)"), start=True, stop=True
                          ).then_inc(inv_spread, 1)

            def project(out, w, mt):
                for kt in range(KT):
                    mm = three_pass(out, w_hi[:, w, kt, mt * P:(mt + 1) * P], w_lo[:, w, kt, mt * P:(mt + 1) * P],
                                    xn_hi[:, kt], xn_lo[:, kt], kt == 0, kt == KT - 1)
                return mm

            def keys(m, mt):
                pe.wait_ge(xn_lo_made, 2 * m + 2)
                project(work[1][:], WK, mt).then_inc(k_mm, 1)

            def queries(m, mt):
                project(work[(2, 1)[mt]][:], WQ, mt).then_inc(q_mm, 1)

            def values(m, i):
                for t in range(2):
                    tok = slice((2 * i + t) * P, (2 * i + t + 1) * P)
                    for kt in range(KT):
                        mm = three_pass(work[i][:, t * D:(t + 1) * D], xn_hi[:, kt, tok], xn_lo[:, kt, tok],
                                        w_hi[:, WV, kt], w_lo[:, WV, kt], kt == 0, kt == KT - 1)
                mm.then_inc(v_mm, 1)

            def attention_out(b, mt):
                if mt == 0:
                    pe.wait_ge(att_lo_made, 2 * b + 2)
                for hh in range(2):
                    mm = three_pass(work[(2, 0)[mt]][:], w_hi[:, WO, hh, mt * P:(mt + 1) * P],
                                    w_lo[:, WO, hh, mt * P:(mt + 1) * P], att_hi[:, hh], att_lo[:, hh],
                                    hh == 0, hh == 1)
                mm.then_inc(wo_mm, 1)

            def score(n, j, par):
                g = SEQS * n + j
                pe.wait_ge(k_masked, g + 1)
                if j == 0:
                    pe.wait_ge(q_out, 2 * n + 2)
                if reaches(g, 2):
                    pe.wait_ge(centred, g - 1)
                for mt in range(KT):
                    mm = pe.matmul(score_bank[j % 2][:, mt * 256:(mt + 1) * 256], q_diag[par][:, mt, j],
                                   k_heads[j % 2][:, mt].rearrange("p h k -> p (h k)"), start=True, stop=True)
                mm.then_inc(scored, 1)

            def turn_probs(n, j):
                g = SEQS * n + j
                pe.wait_ge(exp_made, g + 1)
                if reaches(g, 1):
                    pe.wait_ge(probsT_out, g)
                for c in range(NC):
                    mm = pe.transpose(probs_bank[:, c * P:(c + 1) * P], probs[j % 2][:, c * P:(c + 1) * P], ident[:])
                mm.then_inc(probs_turned, 1)

            def times_values(n, j):
                g = SEQS * n + j
                pe.wait_ge(probsT_out, g + 1)
                if j % 4 == 0:
                    pe.wait_ge(v_out, 2 * n + j // 4 + 1)
                if reaches(g, 1):
                    pe.wait_ge(att_normed, g)
                for c in range(NC):
                    mm = pe.matmul(attended_bank[:, c * 2 * VW:(c + 1) * 2 * VW], probsT[j % 2][:, c * P:(c + 1) * P],
                                   v_diag[:, j, 2 * c:2 * c + 2].rearrange("p a b -> p (a b)"),
                                   start=True, stop=True)
                mm.then_inc(summed, 1)

            def turn_attended(n, j):
                pe.wait_ge(att_normed, SEQS * n + j + 1)
                if j % 4 == 0 and reaches(2 * n + j // 4, 1):
                    pe.wait_ge(att_lo_made, 2 * n + j // 4)
                pe.transpose(attT_bank[:, (j % 4) * P:(j % 4 + 1) * P], attended[j % 2][:], ident[:]
                             ).then_inc(att_turned, 1)

            def linear_work(n, par, j):
                if j == 0:
                    spread_inverse(n + 1)
                    pe.wait_ge(ms_out, n + 2)
                    values(n, 0)
                if j == 1:
                    values(n, 1)
                if j == 2 and exists(n + 2):
                    pe.wait_ge(scaled, 2 * (n + 1) + 2)
                    turn_x(n + 2, par, 0)
                    pe.wait_ge(v_out, 2 * n + 1)
                    turn_x(n + 2, par, 1)
                if j == 3:
                    if exists(n + 1):
                        pe.wait_ge(v_out, 2 * n + 2)
                        keys(n + 1, 0)
                    if reaches(n, 1):
                        if exists(n + 2):
                            pe.wait_ge(res_made, 2 * (n + 2) + 1)
                        else:
                            pe.wait_ge(scaled, 2 * (n + 1) + 2)
                        attention_out(n - 1, 0)
                if j == 4:
                    if reaches(n, 1):
                        if exists(n + 2):
                            pe.wait_ge(res_made, 2 * (n + 2) + 2)
                        else:
                            pe.wait_ge(v_out, 2 * n + 1)
                        attention_out(n - 1, 1)
                    if exists(n + 1):
                        pe.wait_ge(k_out, 2 * (n + 1) + 1)
                        keys(n + 1, 1)
                if j == 5 and exists(n + 1):
                    if reaches(n, 1):
                        pe.wait_ge(gated_made, 2 * (n - 1) + 1)
                    else:
                        pe.wait_ge(res_made, 2 * (n + 2) + 2)
                    queries(n + 1, 0)
                if j == 6 and exists(n + 1):
                    if reaches(n, 1):
                        pe.wait_ge(gated_made, 2 * (n - 1) + 2)
                    mean_square(n + 2)
                if j == 7 and exists(n + 1):
                    pe.wait_ge(k_out, 2 * (n + 1) + 2)
                    queries(n + 1, 1)

            def body(n, half, par):
                for j in range(SEQS):
                    score(n, j, par)
                    linear_work(n, par, j)
                    if reaches(SEQS * n + j, 1):
                        turn_probs(*before(n, j, 1))
                    if reaches(SEQS * n + j, 2):
                        times_values(*before(n, j, 2))
                    if reaches(SEQS * n + j, 3):
                        turn_attended(*before(n, j, 3))

            pe.wait_ge(loaded, 16 * 9)
            pe.wait_ge(consts_set, 1)
            modulation()
            pe.wait_ge(w_split, 2)
            turn_x(0, 0, 0)
            turn_x(0, 0, 1)
            pe.wait_ge(res_made, 2)
            mean_square(0)
            spread_inverse(0)
            pe.wait_ge(ms_out, 1)
            keys(0, 0)
            pe.wait_ge(k_out, 1)
            keys(0, 1)
            pe.wait_ge(scaled, 2)
            queries(0, 0)
            pe.wait_ge(k_out, 2)
            queries(0, 1)
            pe.wait_ge(q_out, 1)
            turn_x(1, 1, 0)
            turn_x(1, 1, 1)
            pe.wait_ge(res_made, 4)
            mean_square(1)
            over_blocks(pe, body)
            turn_probs(NBLK - 1, SEQS - 1)
            times_values(NBLK - 1, SEQS - 2)
            turn_attended(NBLK - 1, SEQS - 3)
            times_values(NBLK - 1, SEQS - 1)
            turn_attended(NBLK - 1, SEQS - 2)
            turn_attended(NBLK - 1, SEQS - 1)
            attention_out(NBLK - 1, 0)
            attention_out(NBLK - 1, 1)

        @block.vector
        def _(dve):
            def token_stats(m, half, par):
                dve.wait_ge(x_loaded[par], 16 * (half + 1))
                if reaches(m, 1):
                    dve.wait_ge(var_made, m)
                for t in range(TILES):
                    op = dve.bn_stats(stats[:, t], xin[par][:, t])
                op.then_inc(stats_made, 1)
                even_mean, odd_mean = stats[:, :, 1], stats[:, :, 4]
                dve.wait_ge(stats_made, m + 1)
                dve.tensor_tensor(merge[:, 0], even_mean, odd_mean, ALU.add)
                dve.tensor_tensor(merge[:, 1], even_mean, odd_mean, ALU.subtract)
                dve.tensor_tensor(merge[:, 2], stats[:, :, 2], stats[:, :, 5], ALU.add).then_inc(merged, 1)
                dve.wait_ge(merged, 2 * m + 1)
                dve.tensor_scalar(mean[par][:], merge[:, 0], 0.5, None, ALU.mult)
                dve.scalar_tensor_tensor(out=merge[:, 3], in0=merge[:, 1], scalar=0.25, in1=merge[:, 1],
                                         op0=ALU.mult, op1=ALU.mult)
                dve.tensor_scalar(merge[:, 4], merge[:, 2], 1.0 / D, LN_EPS, ALU.mult, ALU.add).then_inc(merged, 1)
                dve.wait_ge(merged, 2 * m + 2)
                dve.tensor_tensor(rstd[par][:], merge[:, 3], merge[:, 4], ALU.add).then_inc(var_made, 1)

            def normalise_tokens(m, par):
                dve.wait_ge(rstd_made, m + 1)
                for t in range(TILES):
                    op = dve.tensor_scalar(xin[par][:, t], xin[par][:, t], mean[par][:, t:t + 1],
                                           rstd[par][:, t:t + 1], ALU.subtract, ALU.mult)
                op.then_inc(x_normed, 1)

            def make_residual(m):
                for kt in range(KT):
                    dve.wait_ge(x_turned, 2 * m + kt + 1)
                    dve.scalar_tensor_tensor(out=by_seq(res_block(kt, m)), in0=by_seq(work[(2, 0)[kt]][:]),
                                             scalar=w_sq[:, kt:kt + 1], in1=seq_cols(SHIFT, kt, m),
                                             op0=ALU.mult, op1=ALU.add).then_inc(res_made, 1)

            def mean_square_out(m):
                dve.wait_ge(ms_summed, m + 1)
                if reaches(m, 1):
                    dve.wait_ge(diag_made, m)
                dve.tensor_scalar(mean_sq[:], work[0][:, 0:TILES], RMS_EPS, None, ALU.add).then_inc(ms_out, 1)

            def make_diagonals(m):
                dve.wait_ge(inv_made, m + 1)
                if reaches(m, 1):
                    dve.wait_ge(inv_spread, m)
                for t in range(TILES):
                    op = dve.tensor_scalar(inv_diag[:, t], ident[:], mean_sq[:, t:t + 1], None, ALU.mult)
                op.then_inc(diag_made, 1)

            def scale_by_rms(m):
                dve.wait_ge(inv_spread, m + 1)
                for kt in range(KT):
                    dve.wait_ge(gamma_done, 2 * m + kt + 1)
                    dve.tensor_tensor(normed[:, kt], work[2][:], normed[:, kt], ALU.mult).then_inc(scaled, 1)

            def find_max(n, j):
                dve.wait_ge(scored, SEQS * n + j + 1)
                dve.tensor_reduce(row_max[j % 2][:], score_bank[j % 2][:].rearrange("p (h k) -> p h k", k=SEQ),
                                  AX_X, ALU.max).then_inc(max_made, 1)

            def centre(n, j):
                g = SEQS * n + j
                if reaches(g, 2):
                    dve.wait_ge(probs_turned, g - 1)
                dve.wait_ge(max_made, g + 1)
                dve.tensor_tensor(probs[j % 2][:].rearrange("p (h k) -> p h k", k=SEQ),
                                  score_bank[j % 2][:].rearrange("p (h k) -> p h k", k=SEQ),
                                  row_max[j % 2][:].unsqueeze(2).broadcast_to([P, 8, SEQ]), ALU.subtract
                                  ).then_inc(centred, 1)

            def attended_grid():
                return attended_bank[:, 0:2 * NC * VW].rearrange("p (c h w) -> p c h w", h=2, w=VW)

            def invert_sums(n, j):
                dve.wait_ge(summed, SEQS * n + j + 1)
                dve.reciprocal(inv_sum[j % 2][:].rearrange("p (c h) -> p c h", h=2), attended_grid()[:, :, :, VW - 1]
                               ).then_inc(inv_sum_made, 1)

            def normalise_attended(n, j):
                g = SEQS * n + j
                if reaches(g, 2):
                    dve.wait_ge(att_turned, g - 1)
                dve.wait_ge(inv_sum_made, g + 1)
                for hh in range(2):
                    rows = slice(hh * HALF, (hh + 1) * HALF)
                    op = dve.tensor_tensor(
                        attended[j % 2][rows].rearrange("p (c h d) -> p c h d", c=NC, d=DH),
                        attended_grid()[rows, :, hh, 0:2 * DH].rearrange("p c (h d) -> p c h d", d=DH),
                        inv_sum[j % 2][rows].rearrange("p (c h) -> p c h", h=2).unsqueeze(3)
                        .broadcast_to([HALF, NC, 2, DH]), ALU.mult)
                op.then_inc(att_normed, 1)

            def attended_lo(b, q):
                dve.wait_ge(att_hi_made, 2 * b + q + 1)
                cols = slice(q * BLK // 2, (q + 1) * BLK // 2)
                dve.tensor_tensor(att_lo[:, :, cols].rearrange("p h (s t) -> p h s t", t=SEQ),
                                  attT_bank[:].rearrange("p (s h t) -> p h s t", h=2, t=SEQ),
                                  att_hi[:, :, cols].bitcast(F32).rearrange("p h (s t) -> p h s t", t=SEQ),
                                  ALU.subtract).then_inc(att_lo_made, 1)

            def gate_attention(b, mt):
                dve.wait_ge(wo_mm, 2 * b + mt + 1)
                if reaches(b, 1):
                    dve.wait_ge(resid1_done, 2 * (b - 1) + mt + 1)
                dve.tensor_tensor(by_seq(gated[:, mt]), by_seq(work[(2, 0)[mt]][:]), seq_cols(A_ALPHA, mt, b), ALU.mult
                                  ).then_inc(gated_made, 1)

            def body(n, half, par):
                for j in range(SEQS):
                    if reaches(SEQS * n + j, 3):
                        invert_sums(*before(n, j, 3))
                        normalise_attended(*before(n, j, 3))
                    if j == 3 and reaches(n, 1):
                        attended_lo(n - 1, 1)
                    if j == 7:
                        attended_lo(n, 0)
                    if j == 0 and exists(n + 2):
                        token_stats(n + 2, half + 1, par)
                    find_max(n, j)
                    centre(n, j)
                    if j == 0:
                        scale_by_rms(n + 1)
                    if exists(n + 2):
                        if j == 1:
                            normalise_tokens(n + 2, par)
                        if j == 2:
                            make_residual(n + 2)
                    if j in (4, 5) and reaches(n, 1):
                        gate_attention(n - 1, j - 4)
                    if j == 6 and exists(n + 1):
                        mean_square_out(n + 2)
                    if j == 7 and exists(n + 1):
                        make_diagonals(n + 2)

            dve.wait_ge(loaded, 16 * 9)
            raw = w_raw[:].rearrange("p a b c -> p (a b c)")
            hi = w_hi[:].rearrange("p a b c -> p (a b c)")
            lo = w_lo[:].rearrange("p a b c -> p (a b c)")
            dve.tensor_copy(hi, raw).then_inc(w_split, 1)
            dve.wait_ge(w_split, 1)
            dve.tensor_tensor(lo, raw, hi.bitcast(F32), ALU.subtract).then_inc(w_split, 1)
            dve.tensor_tensor(w_sq[:], vecs[:, LN_W], vecs[:, LN_W], ALU.mult).then_inc(shift_made, 1)
            token_stats(0, 0, 0)
            dve.wait_ge(mod_out, 1)
            for kt in range(KT):
                op = dve.tensor_scalar(mod[:, SHIFT, kt], mod[:, SHIFT, kt], vecs[:, LN_B, kt:kt + 1],
                                       vecs[:, LN_W, kt:kt + 1], ALU.add, ALU.mult)
            op.then_inc(shift_made, 1)
            dve.wait_ge(shift_made, 2)
            for kt in range(KT):
                op = dve.tensor_scalar(mod[:, SHIFT, kt], mod[:, SHIFT, kt], vecs[:, LN_B, kt:kt + 1], None, ALU.add)
            op.then_inc(shift_made, 1)
            normalise_tokens(0, 0)
            dve.wait_ge(shift_made, 3)
            make_residual(0)
            mean_square_out(0)
            make_diagonals(0)
            scale_by_rms(0)
            token_stats(1, 0, 1)
            normalise_tokens(1, 1)
            make_residual(1)
            mean_square_out(1)
            make_diagonals(1)
            over_blocks(dve, body)
            for j in (SEQS - 3, SEQS - 2, SEQS - 1):
                invert_sums(NBLK - 1, j)
                normalise_attended(NBLK - 1, j)
            attended_lo(NBLK - 1, 1)
            gate_attention(NBLK - 1, 0)
            gate_attention(NBLK - 1, 1)

        @block.scalar
        def _(act):
            def square(m):
                if reaches(m, 1):
                    act.wait_ge(ms_summed, m)
                if isinstance(m, int) and m == NBLK:
                    act.wait_ge(resid1_done, 2)
                for kt in range(KT):
                    if exists(m):
                        act.wait_ge(res_made, 2 * m + kt + 1)
                    act.activation(squares[:, kt], res_block(kt, normed_block(m)), ACT.Square).then_inc(squared, 1)

            def split_hi(m):
                if reaches(m, 1):
                    act.wait_ge(v_mm, 2 * m)
                for kt in range(KT):
                    act.wait_ge(xn_made, 2 * m + kt + 1)
                    act.activation(xn_hi[:, kt], normed[:, kt], ACT.Copy).then_inc(xn_hi_made, 1)

            def keys_out(m, par, mt):
                act.wait_ge(k_mm, 2 * m + mt + 1)
                if reaches(m, 2):
                    act.wait_ge(k_masked, SEQS * (m - 1))
                act.activation(keysT[par][:, mt], work[1][:], ACT.Copy).then_inc(k_out, 1)

            def queries_out(m, par, mt):
                act.wait_ge(q_mm, 2 * m + mt + 1)
                if reaches(m, 2):
                    act.wait_ge(scored, SEQS * (m - 1))
                for hh in range(2):
                    rows = slice(hh * HALF, (hh + 1) * HALF)
                    op = act.activation(q_diag[par][rows, mt, :, hh * SEQ:(hh + 1) * SEQ],
                                        by_seq(work[(2, 1)[mt]][rows]), ACT.Copy)
                op.then_inc(q_out, 1)

            def values_out(m, i):
                act.wait_ge(v_mm, 2 * m + i + 1)
                if reaches(m, 1):
                    act.wait_ge(summed, SEQS * (m - 1) + 4 * i + 4)
                for s in range(2):
                    for ho in range(2):
                        src = work[i][s * HALF:(s + 1) * HALF].rearrange("p (t c w) -> p t c w", t=2, w=2 * DH)
                        dst = v_diag[ho * HALF:(ho + 1) * HALF].rearrange("p (t s) c w -> p t s c w", s=2)
                        op = act.activation(dst[:, 2 * i:2 * i + 2, s, :, ho * DH:(ho + 1) * DH],
                                            src[:, :, :, ho * DH:(ho + 1) * DH], ACT.Copy)
                op.then_inc(v_out, 1)

            def exponentials(n, j):
                g = SEQS * n + j
                act.wait_ge(centred, g + 1)
                act.activation(probs[j % 2][:], probs[j % 2][:], ACT.Exp, scale=SCALE).then_inc(exp_made, 1)

            def probs_out(n, j):
                g = SEQS * n + j
                act.wait_ge(probs_turned, g + 1)
                if reaches(g, 2):
                    act.wait_ge(summed, g - 1)
                act.activation(probsT[j % 2][:], probs_bank[:], ACT.Copy).then_inc(probsT_out, 1)

            def attended_hi(b, q):
                act.wait_ge(att_turned, SEQS * b + 4 * q + 4)
                if reaches(b, 1):
                    act.wait_ge(wo_mm, 2 * b)
                cols = slice(q * BLK // 2, (q + 1) * BLK // 2)
                act.activation(att_hi[:, :, cols].rearrange("p h (s t) -> p h s t", t=SEQ),
                               attT_bank[:].rearrange("p (s h t) -> p h s t", h=2, t=SEQ), ACT.Copy
                               ).then_inc(att_hi_made, 1)

            def body(n, half, par):
                for j in range(SEQS):
                    if j == 3 and reaches(n, 1):
                        attended_hi(n - 1, 1)
                    if j == 7:
                        attended_hi(n, 0)
                    if j == 2:
                        split_hi(n + 1)
                    if j == 7 and exists(n + 1):
                        queries_out(n + 1, 1 - par, 1)
                    exponentials(n, j)
                    if reaches(SEQS * n + j, 1):
                        probs_out(*before(n, j, 1))
                    if j in (0, 1):
                        values_out(n, j)
                    if exists(n + 1):
                        if j == 3:
                            square(n + 2)
                        if j in (3, 4):
                            keys_out(n + 1, 1 - par, j - 3)
                        if j == 5:
                            queries_out(n + 1, 1 - par, 0)

            act.wait_ge(loaded, 16 * 9)
            act.wait_ge(mod_mm, 1)
            for kt in range(KT):
                act.activation(mod[:, SHIFT, kt], bank[0][:, kt * P:(kt + 1) * P], ACT.Tanh,
                               bias=vecs[:, LIN_B, kt:kt + 1])
            act.activation(mod[:, 1].rearrange("p k s -> p (k s)"), bank[0][:, 2 * P:4 * P], ACT.Copy)
            for i in range(1, 4):
                width = min(4 * P, 7 * KT * P - 4 * P * i)
                op = act.activation(mod[:].rearrange("p w k s -> p (w k s)")[:, 4 * P * i:4 * P * i + width],
                                    bank[i][:, 0:width], ACT.Copy)
            op.then_inc(mod_out, 1)
            act.wait_ge(consts_set, 1)
            act.wait_ge(diag_cleared, 1)
            square(0)
            split_hi(0)
            keys_out(0, 0, 0)
            keys_out(0, 0, 1)
            queries_out(0, 0, 0)
            queries_out(0, 0, 1)
            square(1)
            over_blocks(act, body)
            probs_out(NBLK - 1, SEQS - 1)
            attended_hi(NBLK - 1, 1)

        @block.gpsimd
        def _(pool):
            def root(out, variance):
                return pool.tensor_tensor(out, variance, minus_half[:], ALU.pow)

            def token_rstd(m, par):
                pool.wait_ge(var_made, m + 1)
                root(rstd[par][:], rstd[par][:]).then_inc(rstd_made, 1)

            def inverse_rms(m):
                pool.wait_ge(ms_out, m + 1)
                root(mean_sq[:], mean_sq[:]).then_inc(inv_made, 1)

            def apply_gamma(m):
                if isinstance(m, int) and m == NBLK:
                    pool.wait_ge(resid1_done, 2)
                if reaches(m, 1):
                    pool.wait_ge(xn_lo_made, 2 * m)
                for kt in range(KT):
                    if exists(m):
                        pool.wait_ge(res_made, 2 * m + kt + 1)
                    pool.tensor_tensor(by_seq(normed[:, kt]), by_seq(res_block(kt, normed_block(m))),
                                       seq_cols(row_for(m, A_GAMMA, F_GAMMA), kt, normed_block(m)), ALU.mult
                                       ).then_inc(gamma_done, 1)

            def apply_beta(m, kt):
                pool.wait_ge(scaled, 2 * m + kt + 1)
                pool.tensor_tensor(by_seq(normed[:, kt]), by_seq(normed[:, kt]),
                                   seq_cols(row_for(m, A_BETA, F_BETA), kt, normed_block(m)), ALU.add
                                   ).then_inc(xn_made, 1)

            def split_lo(m):
                if reaches(m, 1):
                    pool.wait_ge(v_mm, 2 * m)
                for kt in range(KT):
                    pool.wait_ge(xn_hi_made, 2 * m + kt + 1)
                    pool.tensor_tensor(xn_lo[:, kt], normed[:, kt], xn_hi[:, kt].bitcast(F32), ALU.subtract
                                       ).then_inc(xn_lo_made, 1)

            def mask_keys(m, j, par):
                g = SEQS * m + j
                if j == 0:
                    pool.wait_ge(k_out, 2 * m + 2)
                if reaches(g, 2):
                    pool.wait_ge(scored, g - 1)
                pool.tensor_tensor(k_heads[j % 2][:],
                                   keysT[par][:, :, j * SEQ:(j + 1) * SEQ].unsqueeze(2).broadcast_to([P, KT, 4, SEQ]),
                                   mask[:].unsqueeze(1).unsqueeze(3).broadcast_to([P, KT, 4, SEQ]), ALU.mult
                                   ).then_inc(k_masked, 1)

            def add_attention(b, mt):
                pool.wait_ge(gated_made, 2 * b + mt + 1)
                pool.tensor_tensor(res_block(mt, b), res_block(mt, b), gated[:, mt], ALU.add
                                   ).then_inc(resid1_done, 1)

            def body(n, half, par):
                for j in range(SEQS):
                    if j < SEQS - 1:
                        mask_keys(n, j + 1, par)
                    elif exists(n + 1):
                        mask_keys(n + 1, 0, 1 - par)
                    if j == 0 and exists(n + 2):
                        token_rstd(n + 2, par)
                    if j in (0, 1):
                        apply_beta(n + 1, j)
                    if j == 2:
                        split_lo(n + 1)
                    if j == 3 and exists(n + 1):
                        apply_gamma(n + 2)
                    if j in (5, 6) and reaches(n, 1):
                        add_attention(n - 1, j - 5)
                    if j == 6 and exists(n + 1):
                        inverse_rms(n + 2)

            pool.memset(mean_w[:].bitcast(F32), 1.0 / D)
            pool.memset(mean_col[:], 1.0 / D)
            pool.memset(ones[:], 1.0)
            pool.memset(minus_half[:], -0.5)
            pool.memset(eps_rms[:], RMS_EPS).then_inc(consts_set, 1)
            pool.wait_ge(consts_set, 1)
            pool.memset(q_diag[0][:], 0.0)
            pool.memset(v_diag[:], 0.0).then_inc(v_cleared, 1)
            pool.wait_ge(v_cleared, 1)
            for ho in range(2):
                grid = v_diag[ho * HALF:(ho + 1) * HALF].rearrange("p s (c h) w -> p (s c) h w", h=2)
                pool.memset(grid[:, :, ho, VW - 1], 1.0).then_inc(v_cleared, 1)
                pool.wait_ge(v_cleared, ho + 2)
            pool.wait_ge(w_split, 2)
            pool.memset(q_diag[1][:], 0.0).then_inc(diag_cleared, 1)
            pool.wait_ge(loaded, 16 * 9)
            pool.wait_ge(mod_out, 1)
            token_rstd(0, 0)
            apply_gamma(0)
            inverse_rms(0)
            apply_beta(0, 0)
            apply_beta(0, 1)
            split_lo(0)
            token_rstd(1, 1)
            pool.wait_ge(mod_mm, 1)
            mask_keys(0, 0, 0)
            apply_gamma(1)
            inverse_rms(1)
            over_blocks(pool, body)
            add_attention(NBLK - 1, 0)
            add_attention(NBLK - 1, 1)


def phase2(nc, outer, bank, x_res, mod, vecs, mean_w, eps_rms, normed, xn_hi_0, xn_lo_0, ffn_raw, out_t):
    LAG = 2
    RING = 4
    with ExitStack() as ctx:
        def sb(name, shape, dt=F32):
            return ctx.enter_context(nc.sbuf_tensor(name, shape, dt))

        def sem(name):
            return outer.enter_context(nc.semaphore(name))

        gate_bank, hidden_bank, y_bank, ms_bank = bank[0:2], bank[2:4], bank[4:6], bank[6]

        w_hi = sb("ffn_hi", [P, 3, KT * HID], F32R)
        w_lo = sb("ffn_lo", [P, 3, KT * HID], F32R)
        squares = sb("squares2", [P, KT, BLK])
        sq_hi = sb("sq_hi", [P, KT, BLK], F32R)
        sq_lo = sb("sq_lo", [P, KT, BLK], F32R)
        inv_rms = sb("inv_rms2", [P, BLK])
        xn_hi = [xn_hi_0, sb("xn_hi_1", [P, KT, BLK], F32R)]
        xn_lo = [xn_lo_0, sb("xn_lo_1", [P, KT, BLK], F32R)]
        silu = [sb(f"silu{i}", [P, BLK]) for i in range(2)]
        prod = [sb(f"prod{i}", [P, BLK]) for i in range(2)]
        prod_hi = [sb(f"prod_hi{i}", [P, BLK], F32R) for i in range(RING)]
        prod_lo = [sb(f"prod_lo{i}", [P, BLK], F32R) for i in range(RING)]
        gated = sb("gated2", [P, KT, BLK])

        up_hi_made, up_lo_made = sem("up_hi_made"), sem("up_lo_made")
        down_hi_made, down_lo_made = sem("down_hi_made"), sem("down_lo_made")
        squared = sem("squared2")
        sq_hi_made = sem("sq_hi_made")
        sq_lo_made = sem("sq_lo_made")
        ms_summed = sem("ms_summed2")
        rms_made = sem("rms_made2")
        inv_made = sem("inv_made2")
        gamma_done = sem("gamma_done2")
        scaled = sem("scaled2")
        xn_made = sem("xn_made2")
        xn_hi_made = sem("xn_hi_made2")
        xn_lo_made = sem("xn_lo_made2")
        gate_mm, hidden_mm = sem("gate_mm"), sem("hidden_mm")
        silu_made = sem("silu_made")
        prod_made = sem("prod_made")
        prod_hi_made = sem("prod_hi_made")
        prod_lo_made = sem("prod_lo_made")
        out_mm = sem("out_mm")
        gated_made = sem("gated_made2")
        y_made = sem("y_made")
        stored = sem("stored")

        block = ctx.enter_context(nc.Block())

        def seq_cols(table_row, kt, n):
            return mod[:, table_row, kt, bass.ds(n * SEQS, SEQS)].unsqueeze(2).broadcast_to([P, SEQS, SEQ])

        def by_seq(ap):
            return ap.rearrange("p (s t) -> p s t", t=SEQ)

        def res_block(kt, n):
            return x_res[:, kt, bass.ds(n * BLK, BLK)]

        def up_weights(w, t):
            return w[:, 0:2].rearrange("p w (k h) -> p w k h", k=KT)[:, :, :, t * P:(t + 1) * P]

        def down_weights(w, t):
            return w[:, 2, t * D:(t + 1) * D]

        @block.tensor
        def _(pe):
            def mean_square(m):
                pe.wait_ge(sq_lo_made, 2 * m)
                if reaches(m, 2):
                    pe.wait_ge(rms_made, m - 1)
                for i, part in enumerate((sq_hi, sq_lo)):
                    for kt in range(KT):
                        mm = pe.matmul(ms_bank[:], mean_w[:], part[:, kt], start=(i + kt == 0),
                                       stop=(i == 1 and kt == KT - 1))
                mm.then_inc(ms_summed, 1)

            def up(out, which, t, par):
                for kt in range(KT):
                    cols = slice(kt * HID + t * P, kt * HID + (t + 1) * P)
                    pe.matmul(out, w_hi[:, which, cols], xn_hi[par][:, kt], start=(kt == 0), stop=False)
                    pe.matmul(out, w_hi[:, which, cols], xn_lo[par][:, kt], start=False, stop=False)
                    mm = pe.matmul(out, w_lo[:, which, cols], xn_hi[par][:, kt], start=False, stop=(kt == KT - 1))
                return mm

            def down(n, t):
                if not reaches(n, 1):
                    pe.wait_ge(down_lo_made, t + 1)
                pe.wait_ge(prod_lo_made, HT * n + t + 1)
                if t == 0 and reaches(n, 1):
                    pe.wait_ge(gated_made, 2 * n)
                for mt in range(KT):
                    cols = slice(t * D + mt * P, t * D + (mt + 1) * P)
                    pe.matmul(y_bank[mt][:], w_hi[:, 2, cols], prod_hi[t % RING][:], start=(t == 0), stop=False)
                    pe.matmul(y_bank[mt][:], w_hi[:, 2, cols], prod_lo[t % RING][:], start=False, stop=False)
                    mm = pe.matmul(y_bank[mt][:], w_lo[:, 2, cols], prod_hi[t % RING][:], start=False,
                                   stop=(t == HT - 1))
                mm.then_inc(out_mm, 1)

            def body(n, half, par):
                if reaches(n, 1):
                    pe.wait_ge(xn_lo_made, 2 * n)
                for t in range(HT):
                    if not reaches(n, 1):
                        pe.wait_ge(up_lo_made, t + 1)
                    early = not reaches(HT * n + t, 2)
                    if not early:
                        pe.wait_ge(silu_made, HT * n + t - 1)
                    up(gate_bank[t % 2][:], 0, t, par).then_inc(gate_mm, 1)
                    if not early:
                        pe.wait_ge(prod_made, HT * n + t - 1)
                    up(hidden_bank[t % 2][:], 1, t, par).then_inc(hidden_mm, 1)
                    if t >= LAG:
                        down(n, t - LAG)
                    elif reaches(n, 1):
                        down(n - 1, t - LAG + HT)
                    if t == 2 and exists(n + 1):
                        mean_square(n + 1)

            over_blocks(pe, body)
            down(NBLK - 1, HT - 2)
            down(NBLK - 1, HT - 1)

        @block.scalar
        def _(act):
            def split_up(t):
                act.activation(up_weights(w_hi, t), up_weights(ffn_raw, t), ACT.Copy).then_inc(up_hi_made, 1)

            def split_down(t):
                act.activation(down_weights(w_hi, t), down_weights(ffn_raw, t), ACT.Copy).then_inc(down_hi_made, 1)

            def square(m):
                if reaches(m, 2):
                    act.wait_ge(sq_lo_made, 2 * (m - 1))
                for kt in range(KT):
                    act.activation(squares[:, kt], res_block(kt, m), ACT.Square).then_inc(squared, 1)
                if reaches(m, 2):
                    act.wait_ge(ms_summed, m - 1)
                for kt in range(KT):
                    act.wait_ge(squared, 2 * (m - 1) + kt + 1)
                    act.activation(sq_hi[:, kt], squares[:, kt], ACT.Copy).then_inc(sq_hi_made, 1)

            def root_mean_square(m):
                act.wait_ge(ms_summed, m)
                if reaches(m, 2):
                    act.wait_ge(scaled, 2 * (m - 1))
                act.activation(inv_rms[:], ms_bank[:], ACT.Sqrt, bias=eps_rms[:]).then_inc(rms_made, 1)

            def split_hi(m, par):
                if reaches(m, 2):
                    act.wait_ge(hidden_mm, HT * (m - 1))
                for kt in range(KT):
                    act.wait_ge(xn_made, 2 * (m - 1) + kt + 1)
                    act.activation(xn_hi[par][:, kt], normed[:, kt], ACT.Copy).then_inc(xn_hi_made, 1)

            def gate(n, t):
                act.wait_ge(gate_mm, HT * n + t + 1)
                if reaches(HT * n + t, 2):
                    act.wait_ge(prod_made, HT * n + t - 1)
                act.activation(silu[t % 2][:], gate_bank[t % 2][:], ACT.Silu).then_inc(silu_made, 1)

            def product_hi(n, t):
                act.wait_ge(prod_made, HT * n + t + 1)
                if reaches(HT * n + t, RING):
                    act.wait_ge(out_mm, HT * n + t - RING + 1)
                act.activation(prod_hi[t % RING][:], prod[t % 2][:], ACT.Copy).then_inc(prod_hi_made, 1)

            def body(n, half, par):
                for t in range(HT):
                    gate(n, t)
                    if not reaches(n, 1):
                        if t + 2 < HT:
                            split_up(t + 2)
                        split_down(t)
                    product_hi(n, t)
                    if t == 0 and exists(n + 1):
                        square(n + 1)
                    if t == 2 and exists(n + 1):
                        root_mean_square(n + 1)
                    if t == 4 and exists(n + 1):
                        split_hi(n + 1, 1 - par)

            split_up(0)
            split_up(1)
            over_blocks(act, body)

        @block.vector
        def _(dve):
            def split_up(t):
                dve.wait_ge(up_hi_made, t + 1)
                dve.tensor_tensor(up_weights(w_lo, t), up_weights(ffn_raw, t), up_weights(w_hi, t).bitcast(F32),
                                  ALU.subtract).then_inc(up_lo_made, 1)

            def split_down(t):
                dve.wait_ge(down_hi_made, t + 1)
                dve.tensor_tensor(down_weights(w_lo, t), down_weights(ffn_raw, t), down_weights(w_hi, t).bitcast(F32),
                                  ALU.subtract).then_inc(down_lo_made, 1)

            def squares_lo(m):
                if reaches(m, 2):
                    dve.wait_ge(ms_summed, m - 1)
                for kt in range(KT):
                    dve.wait_ge(sq_hi_made, 2 * (m - 1) + kt + 1)
                    dve.tensor_tensor(sq_lo[:, kt], squares[:, kt], sq_hi[:, kt].bitcast(F32), ALU.subtract
                                      ).then_inc(sq_lo_made, 1)

            def invert_rms(m):
                dve.wait_ge(rms_made, m)
                dve.reciprocal(inv_rms[:], inv_rms[:]).then_inc(inv_made, 1)
                dve.wait_ge(inv_made, m)
                for kt in range(KT):
                    dve.wait_ge(gamma_done, 2 * (m - 1) + kt + 1)
                    dve.tensor_tensor(normed[:, kt], normed[:, kt], inv_rms[:], ALU.mult).then_inc(scaled, 1)

            def split_lo(m, par):
                if reaches(m, 2):
                    dve.wait_ge(hidden_mm, HT * (m - 1))
                for kt in range(KT):
                    dve.wait_ge(xn_hi_made, 2 * (m - 1) + kt + 1)
                    dve.tensor_tensor(xn_lo[par][:, kt], normed[:, kt], xn_hi[par][:, kt].bitcast(F32),
                                      ALU.subtract).then_inc(xn_lo_made, 1)

            def product(n, t):
                dve.wait_ge(silu_made, HT * n + t + 1)
                dve.wait_ge(hidden_mm, HT * n + t + 1)
                if reaches(HT * n + t, 2):
                    dve.wait_ge(prod_lo_made, HT * n + t - 1)
                dve.tensor_tensor(prod[t % 2][:], hidden_bank[t % 2][:], silu[t % 2][:], ALU.mult
                                  ).then_inc(prod_made, 1)

            def product_lo(n, t):
                dve.wait_ge(prod_hi_made, HT * n + t + 1)
                if reaches(HT * n + t, RING):
                    dve.wait_ge(out_mm, HT * n + t - RING + 1)
                dve.tensor_tensor(prod_lo[t % RING][:], prod[t % 2][:], prod_hi[t % RING][:].bitcast(F32),
                                  ALU.subtract).then_inc(prod_lo_made, 1)

            def gate_ffn(b):
                dve.wait_ge(out_mm, HT * (b + 1))
                if reaches(b, 1):
                    dve.wait_ge(y_made, 2 * b)
                for mt in range(KT):
                    dve.scalar_tensor_tensor(out=by_seq(gated[:, mt]), in0=by_seq(y_bank[mt][:]),
                                             scalar=vecs[:, OUT_B, mt:mt + 1], in1=seq_cols(F_ALPHA, mt, b),
                                             op0=ALU.add, op1=ALU.mult).then_inc(gated_made, 1)

            def body(n, half, par):
                for t in range(HT):
                    product(n, t)
                    if not reaches(n, 1):
                        if t + 2 < HT:
                            split_up(t + 2)
                        split_down(t)
                    product_lo(n, t)
                    if t == 0 and exists(n + 1):
                        squares_lo(n + 1)
                    if t == 1 and reaches(n, 1):
                        gate_ffn(n - 1)
                    if t == 3 and exists(n + 1):
                        invert_rms(n + 1)
                    if t == 4 and exists(n + 1):
                        split_lo(n + 1, 1 - par)

            split_up(0)
            split_up(1)
            over_blocks(dve, body)
            gate_ffn(NBLK - 1)

        @block.gpsimd
        def _(pool):
            def apply_gamma(m):
                if reaches(m, 2):
                    pool.wait_ge(xn_lo_made, 2 * (m - 1))
                for kt in range(KT):
                    pool.tensor_tensor(by_seq(normed[:, kt]), by_seq(res_block(kt, m)), seq_cols(F_GAMMA, kt, m),
                                       ALU.mult).then_inc(gamma_done, 1)

            def apply_beta(m):
                for kt in range(KT):
                    pool.wait_ge(scaled, 2 * (m - 1) + kt + 1)
                    pool.tensor_tensor(by_seq(normed[:, kt]), by_seq(normed[:, kt]), seq_cols(F_BETA, kt, m),
                                       ALU.add).then_inc(xn_made, 1)

            def add_ffn(b):
                for mt in range(KT):
                    pool.wait_ge(gated_made, 2 * b + mt + 1)
                    pool.tensor_tensor(res_block(mt, b), res_block(mt, b), gated[:, mt], ALU.add
                                       ).then_inc(y_made, 1)

            def body(n, half, par):
                if exists(n + 1):
                    apply_gamma(n + 1)
                if reaches(n, 1):
                    add_ffn(n - 1)
                if exists(n + 1):
                    apply_beta(n + 1)

            over_blocks(pool, body)
            add_ffn(NBLK - 1)

        @block.sync
        def _(sp):
            def store(n):
                for kt in range(KT):
                    sp.wait_ge(y_made, 2 * n + kt + 1)
                    sp.dma_start(out_t[kt * P:(kt + 1) * P, bass.ds(n * BLK, BLK)], res_block(kt, n)
                                 ).then_inc(stored, 16)

            with sp.Fori(0, NBLK) as n:
                store(n)
            sp.wait_ge(stored, 16 * KT * NBLK)


def kernel(**inputs):
    import numpy as np
    import concourse.bacc as bacc
    from concourse import mybir as mb
    from concourse.bass_utils import run_bass_kernel_spmd

    a = {k: np.asarray(v) for k, v in inputs.items()}
    f = {k[len("L1_cond_"):]: v for k, v in a.items() if k.startswith("L1_cond_")}
    by_partition = lambda v: v.reshape(KT, P).T
    split_heads = lambda w: w.reshape(2, 2, 2, 2, DH, D)
    wv = split_heads(f["W_v"]).transpose(0, 2, 1, 3, 4, 5).reshape(D, D)
    wo = split_heads(f["W_o"].T).transpose(1, 0, 2, 3, 4, 5).reshape(D, D)
    mod_rows = [a["L0_cond_lin_w"], f["attn_gamma_w"], f["attn_beta_w"], f["attn_alpha_w"],
                f["ffn_gamma_w"], f["ffn_beta_w"], f["ffn_alpha_w"]]
    features = np.arange(P)
    arrays = {
        "x": a["x"].reshape(TOKENS, D),
        "cond_t": a["cond_256"].T,
        "mod_w": np.stack([w.T for w in mod_rows]),
        "feat_vecs": np.stack([by_partition(v) for v in
                               (a["L0_cond_weight"], a["L0_cond_bias"], a["L0_cond_lin_b"], f["out_b"])], axis=1),
        "attn_w": np.stack([f["W_q"].T, f["W_k"].T, wv.T, wo]),
        "gate_w": f["gate_w"].T,
        "hidden_w": f["hidden_w"].T,
        "out_w": f["out_w"].T,
        "identity": np.eye(P, dtype=np.float32),
        "head_mask": (features[:, None] % HALF // DH == np.arange(4)[None, :]).astype(np.float32),
    }
    nc = bacc.Bacc("TRN2", target_bir_lowering=False, num_devices=1)
    args, feeds = [], {}
    for name, v in arrays.items():
        v = np.ascontiguousarray(v)
        feeds[f"{name}_dram"] = v
        args.append(nc.dram_tensor(f"{name}_dram", v.shape, mb.dt.from_np(v.dtype), kind="ExternalInput").ap())
    args.append(nc.dram_tensor("out_t_dram", (D, TOKENS), F32, kind="ExternalOutput").ap())
    conditioned_block(nc, *args)
    r = run_bass_kernel_spmd(nc, [feeds], core_ids=[0])
    got = r.results[0]["out_t_dram"]
    return np.ascontiguousarray(got.T).reshape(BATCH, SEQ, D)
```
